# Optimizing a Trainium2 kernel written in Bass

```python
import numpy as np
import jax
import jax.numpy as jnp

def _softmax(x, axis=-1):
    return jax.nn.softmax(x, axis=axis)

def _gelu(x):
    return jax.nn.gelu(x, approximate=True)

def _silu(x):
    return jax.nn.silu(x)

def _sigmoid(x):
    return jax.nn.sigmoid(x)

def _layernorm(x, axis=-1, eps=1e-05):
    m = jnp.mean(x, axis=axis, keepdims=True)
    v = jnp.var(x, axis=axis, keepdims=True)
    return (x - m) / jnp.sqrt(v + eps)

def _scatter_add(tgt, idx, src, axis=0):
    return tgt.at[idx].add(src)

def _segment_sum(src, seg, n):
    return jax.ops.segment_sum(src, seg, n)
kernel_name = 'mk_adj_resnorm_d2_adj_r2_ed4ddd'

def setup_inputs(seed: int=0):
    np.random.seed(seed)
    _w = jnp.asarray

    def _rec_inputs():
        import jax
        import jax.numpy as jnp
        _gk = jax.random.key(seed)
        x = 7.22e-05 + 1 * jax.random.normal(jax.random.fold_in(_gk, 1), (16, 512, 128), jnp.float32)
        _a = jax.random.bernoulli(jax.random.fold_in(_gk, 2), 0.03125, (512, 512))
        _a = jnp.logical_or(_a, jnp.swapaxes(_a, -1, -2))
        _a = jnp.logical_or(_a, jnp.eye(512, dtype=bool))
        _af = _a.astype(jnp.float32)
        _af = _af * jax.random.uniform(jax.random.fold_in(_gk, 3), (512, 512), jnp.float32, 0.05, 0.000976562)
        adj = _af
        return (x, adj)
    x, adj = _rec_inputs()

    def _L0_gnn_setup():
        import jax, jax.numpy as jnp
        import numpy as np
        N_STEPS = 8
        SPATIAL_SCALE = 1.0
        key = jax.random.key(seed)
        ks = jax.random.split(key, 6)
        B, N, D = (32, 512, 128)
        x = jax.random.normal(ks[0], (B, N, D), dtype=jnp.float32)
        adj_mx = jax.random.uniform(ks[1], (N, N), dtype=jnp.float32) / N
        alpha_train = jnp.ones((N,), dtype=jnp.float32)
        w = jnp.eye(D, dtype=jnp.float32) + 0.01 * jax.random.normal(ks[2], (D, D), dtype=jnp.float32)
        d = jax.random.uniform(ks[3], (D,), dtype=jnp.float32)
        fc_in_w = jax.random.normal(ks[4], (D, D), dtype=jnp.float32) * (1.0 / np.sqrt(D))
        fc_in_b = jnp.zeros((D,), dtype=jnp.float32)
        return {'x': x, 'adj_mx': adj_mx, 'alpha_train': alpha_train, 'w': w, 'd': d, 'fc_in_w': fc_in_w, 'fc_in_b': fc_in_b, 'vt': 0}
    _L0_gnn_all = _L0_gnn_setup()
    _L0_gnn_in = {k: v for k, v in _L0_gnn_all.items() if k in ('alpha_train', 'w', 'd', 'fc_in_w', 'fc_in_b')}
    del _L0_gnn_all

    def _L1_gnn_setup():
        import jax, jax.numpy as jnp
        import numpy as np
        B, N, H, OUT, RANK = (64, 512, 128, 128, 10)
        ORDER = 2

        def _conv(x, adj):
            return x * jnp.sum(adj, axis=1)[None, :, None]
        key = jax.random.key(seed)
        ks = jax.random.split(key, 6)
        x = jax.random.normal(ks[0], (B, N, H), dtype=jnp.float32)
        support0 = jax.random.uniform(ks[1], (N, N), dtype=jnp.float32)
        support1 = jax.random.uniform(ks[2], (N, N), dtype=jnp.float32)
        node_vec1 = jax.random.normal(ks[3], (N, RANK), dtype=jnp.float32)
        node_vec2 = jax.random.normal(ks[4], (RANK, N), dtype=jnp.float32)
        d_in = (ORDER * 3 + 1) * H
        W = jax.random.normal(ks[5], (d_in, OUT), dtype=jnp.float32) * (1.0 / np.sqrt(d_in))
        b = jnp.zeros((OUT,), dtype=jnp.float32)
        return {'x': x, 'support0': support0, 'support1': support1, 'node_vec1': node_vec1, 'node_vec2': node_vec2, 'W': W, 'b': b}
    _L1_gnn_all = _L1_gnn_setup()
    _L1_gnn_in = {k: v for k, v in _L1_gnn_all.items() if k in ('node_vec1', 'node_vec2', 'W', 'b')}
    del _L1_gnn_all
    return {'x': x, 'adj': adj, 'L0_gnn_alpha_train': _L0_gnn_in['alpha_train'], 'L0_gnn_w': _L0_gnn_in['w'], 'L0_gnn_d': _L0_gnn_in['d'], 'L0_gnn_fc_in_w': _L0_gnn_in['fc_in_w'], 'L0_gnn_fc_in_b': _L0_gnn_in['fc_in_b'], 'L1_gnn_node_vec1': _L1_gnn_in['node_vec1'], 'L1_gnn_node_vec2': _L1_gnn_in['node_vec2'], 'L1_gnn_W': _L1_gnn_in['W'], 'L1_gnn_b': _L1_gnn_in['b']}

def reference(x, adj, L0_gnn_alpha_train, L0_gnn_w, L0_gnn_d, L0_gnn_fc_in_w, L0_gnn_fc_in_b, L1_gnn_node_vec1, L1_gnn_node_vec2, L1_gnn_W, L1_gnn_b):
    import jax
    import jax.numpy as jnp

    def _L0_gnn_ref(x, adj_mx, alpha_train, w, d, fc_in_w, fc_in_b, vt):
        import jax, jax.numpy as jnp
        import numpy as np
        N_STEPS = 8
        SPATIAL_SCALE = 1.0
        x0 = jax.lax.stop_gradient(x)
        h = jnp.einsum('bnd,ed->bne', x, fc_in_w) + fc_in_b
        alph = jax.nn.sigmoid(alpha_train)[:, None]
        d_clamped = jnp.clip(d, 0.0, 1.0)
        w_eff = w * d_clamped @ w.T
        dt = jnp.float32(SPATIAL_SCALE / N_STEPS)

        def euler_step(h, _):
            ax = jnp.einsum('nm,bmd->bnd', adj_mx, h)
            f = alph * 0.5 * (ax - h) + h @ w_eff - h + x0
            return (h + dt * f, None)
        h, _ = jax.lax.scan(euler_step, h, None, length=N_STEPS)
        return h

    def _L1_gnn_ref(x, support0, support1, node_vec1, node_vec2, W, b):
        import jax, jax.numpy as jnp
        import numpy as np
        B, N, H, OUT, RANK = (64, 512, 128, 128, 10)
        ORDER = 2

        def _conv(x, adj):
            return x * jnp.sum(adj, axis=1)[None, :, None]
        adaptive = jax.nn.softmax(jax.nn.relu(node_vec1 @ node_vec2), axis=1)
        outputs = [x]
        for adj in (support0, support1, adaptive):
            x1 = _conv(x, adj)
            outputs.append(x1)
            for _ in range(2, ORDER + 1):
                x1 = _conv(x1, adj)
                outputs.append(x1)
        out = jnp.concatenate(outputs, axis=2)
        out = out @ W + b
        return out
    x = _layernorm(x + _L0_gnn_ref(x, adj, L0_gnn_alpha_train, L0_gnn_w, L0_gnn_d, L0_gnn_fc_in_w, L0_gnn_fc_in_b, 0), axis=-1)
    x = _layernorm(x + _L1_gnn_ref(x, adj, adj, L1_gnn_node_vec1, L1_gnn_node_vec2, L1_gnn_W, L1_gnn_b), axis=-1)
    return x

_drawn_inputs = setup_inputs


def setup_inputs(seed=0):
    import zlib

    import numpy as np

    out = dict(_drawn_inputs(seed))
    spreads = {'L0_gnn_alpha_train': (1.0, 0.6), 'L0_gnn_fc_in_b': (0.0, 0.1), 'L1_gnn_b': (0.0, 0.1)}
    factors = {'L1_gnn_node_vec1': 200.0, 'L1_gnn_node_vec2': 200.0}
    for name, (base, spread) in spreads.items():
        noise = np.random.default_rng([zlib.crc32(name.encode()), seed]).standard_normal(out[name].shape)
        drawn = base * np.exp(spread * noise) if base else spread * noise
        out[name] = jnp.asarray(drawn.astype(out[name].dtype))
    for name, factor in factors.items():
        out[name] = (out[name] * factor).astype(out[name].dtype)
    return out
```

```python
import concourse.bass as bass
from concourse import mybir
from contextlib import ExitStack
from math import comb


def graph_resnorm_kernel(nc, x, xT, adj, alpha, wT, dvec, fcw, bin_, nv1T, nv2, W, bout, out):
    F32 = mybir.dt.float32
    F32R = mybir.dt.float32r
    ALU = mybir.AluOpType
    ACT = mybir.ActivationFunctionType
    AX = mybir.AxisListType

    P = nc.NUM_PARTITIONS
    B, N, D = x.shape
    NT = N // P
    GB = 4
    G = B // GB
    RANK = nv1T.shape[0]
    STEPS = 8
    DT = 1.0 / STEPS
    EPS = 1e-5
    I3 = J3 = 3
    NP5 = 5
    PW = 3 * D
    NV = 4

    ctx = ExitStack()
    with ctx:
        def sb(name, shape, dt=F32):
            return ctx.enter_context(nc.sbuf_tensor(name, shape, dt))

        def pb(name, shape, dt=F32):
            return ctx.enter_context(nc.psum_tensor(name, shape, dt))

        def sem(name):
            return ctx.enter_context(nc.semaphore(name))

        def f32(ap):
            return ap.bitcast(F32)

        ident = sb("ident", [P, P])
        identdt = sb("identdt", [P, P])
        TA = [[sb(f"A{k}T_{part}", [P, NT, N], F32R) for part in ("hi", "lo")] for k in (1, 2, 3)]
        RC = [sb(f"R_{part}", [P, I3, J3 * D], F32R) for part in ("hi", "lo")]
        WC = [sb(f"WP_{part}", [P, NP5 * D], F32R) for part in ("hi", "lo")]
        wp = sb("wp", [P, NP5, D])
        wp_more = sb("wp_more", [P, 2, D])
        bias_out = sb("bias_out", [P, 2, D])
        g_bias = sb("g_bias", [P, NT, D])
        s1 = sb("s1", [P, NT])
        s2 = sb("s2", [P, NT])
        a1 = sb("a1", [P, NT])
        a2 = sb("a2", [P, NT])
        eps_c = sb("eps_c", [P, 1])
        x_in = sb("x_in", [P, GB, NT * D])
        xt_in = sb("xt_in", [P, GB, N])
        xs = [sb(f"x_{part}", [P, 2, NT, D], F32R) for part in ("hi", "lo")]
        yT = [[sb(f"y{i}T_{part}", [P, 2, N], F32R) for part in ("hi", "lo")] for i in range(I3)]
        Z0 = sb("Z0", [P, NT, GB, D])
        Z1 = sb("Z1", [P, NT, GB, D])
        Z2 = [sb(f"Z2_{part}", [P, NT, GB * D], F32R) for part in ("hi", "lo")]
        U = [sb(f"U_{part}", [P, NT, GB * D], F32R) for part in ("hi", "lo")]
        x2 = sb("x2", [P, NT, GB, D])
        x2T = [sb(f"x2T_{part}", [P, GB, D], F32R) for part in ("hi", "lo")]
        res = sb("res", [P, 2, GB, D])
        outb = sb("outb", [P, 2, GB, D])
        LN = [dict({"st": sb(f"st{l}", [P, 2, GB, 6])},
                   **{name: sb(f"{name}{l}", [P, 2, GB]) for name in (
                       "msum", "mdif", "m2", "mean", "within", "between", "ve", "sd", "r0", "q", "q2", "r", "nb")})
              for l in (1, 2)]
        alpha_in = sb("alpha_in", [P, NT])
        esum = sb("esum", [P, NT, 4])
        gcol = sb("gcol", [P, NT])
        ccol = sb("ccol", [P, NT])
        dcol = sb("dcol", [P, 2])
        wT_in = sb("wT_in", [P, D])
        wTs = sb("wTs", [P, D])
        fcw_in = sb("fcw_in", [P, D])
        b_in = sb("b_in", [P, 1])
        CP = sb("CP", [P, STEPS + 1, D])
        RF = sb("RF", [P, I3, J3, D])
        Qc = sb("Qc", [P, I3 * NV])
        Q12 = sb("Q12", [I3 * NV, D])
        V = sb("V", [P, NT, I3 * NV])
        Vs = [sb(f"V_{part}", [P, I3, NT, NV], F32R) for part in ("hi", "lo")]
        V12 = sb("V12", [I3 * NV, NT, P])
        nv1_in = sb("nv1_in", [RANK, NT, P])
        nv2_in = sb("nv2_in", [RANK, N])
        zmax = sb("zmax", [P, NT])
        zneg = sb("zneg", [P, NT])
        zsum = sb("zsum", [P, NT])
        zrec = sb("zrec", [P, NT])
        prob = res[:, :, :, :].rearrange("p s b d -> p s (b d)")
        adj_in = x2[:, :, :, :].rearrange("p t b d -> p t (b d)")
        A = Z0[:, :, :, :].rearrange("p t b d -> p t (b d)")
        As = U
        relu = sb("relu", [P, N])

        left = [pb(f"left{i}", [P, 512]) for i in range(2)]
        right = [pb(f"right{i}", [P, 512]) for i in range(2)]
        turn = pb("turn", [P, 512])
        wide = pb("wide", [P, 2, 512])
        tail = pb("tail", [P, 512])
        tail_v = tail[:, :].rearrange("p (t c) -> p t c", t=2)

        adj_loaded, w_loaded, d_loaded, fcw_loaded, b_loaded = map(
            sem, ("adj_loaded", "w_loaded", "d_loaded", "fcw_loaded", "b_loaded"))
        alpha_loaded, nv_loaded, wp_loaded, bout_loaded = map(
            sem, ("alpha_loaded", "nv_loaded", "wp_loaded", "bout_loaded"))
        ident_step, gate_exp, gate_step, d_step, a_step = map(
            sem, ("ident_step", "gate_exp", "gate_step", "d_step", "a_step"))
        a_high, a_low, at_turned, t_high, t_low, t_made = map(
            sem, ("a_high", "a_low", "at_turned", "t_high", "t_low", "t_made"))
        cp_made, cp_copied, fc_made, r_level, rc_high, rc_low = map(
            sem, ("cp_made", "cp_copied", "fc_made", "r_level", "rc_high", "rc_low"))
        q_made, q_scaled, q_turned, q_copied = map(sem, ("q_made", "q_scaled", "q_turned", "q_copied"))
        v_step, v_made, v_turned, v_copied, gb_made, gb_copied = map(
            sem, ("v_step", "v_made", "v_turned", "v_copied", "gb_made", "gb_copied"))
        wp_step, wc_high, wc_low = map(sem, ("wp_step", "wc_high", "wc_low"))
        z_made, relu_done, zneg_done, z_exp, zrec_done, a_done, coef_done = map(
            sem, ("z_made", "relu_done", "zneg_done", "z_exp", "zrec_done", "a_done", "coef_done"))
        rowsum_done = sem("rowsum_done")
        x_loaded = [sem(f"x_loaded{i}") for i in range(GB)]
        xt_loaded = [sem(f"xt_loaded{i}") for i in range(GB)]
        xs_high, xs_low, xts_high, xts_low = map(sem, ("xs_high", "xs_low", "xts_high", "xts_low"))
        y_made, o1_made, o2_made, left_drained, yT_high = map(
            sem, ("y_made", "o1_made", "o2_made", "left_drained", "yT_high"))
        right_made, inner_mid, inner_base, inner_low = map(
            sem, ("right_made", "inner_mid", "inner_base", "inner_low"))
        u_high, u_low, base_full = map(sem, ("u_high", "u_low", "base_full"))
        ln1_stat, ln1_root, ln1_norm, x2_ready, turn_made, x2T_high, x2T_low = map(
            sem, ("ln1_stat", "ln1_root", "ln1_norm", "x2_ready", "turn_made", "x2T_high", "x2T_low"))
        wide_made, mixed, ln2_stat, ln2_root, ln2_norm, out_ready = map(
            sem, ("wide_made", "mixed", "ln2_stat", "ln2_root", "ln2_norm", "out_ready"))
        slot_free = [sem(f"slot_free{i}") for i in range(2)]
        MIX = 5
        STAT = 4
        NORM1 = 4
        NORM2 = 5

        FIRST = [("splitx", 0), ("splitxT", 0), ("y1", 0), ("y2", 0), ("splitx", 1), ("splitxT", 1),
                 ("y1", 1), ("y2", 1), ("R", 0, 0), ("R", 0, 1), ("R", 0, 2), ("R", 0, 3),
                 ("splitx", 2), ("splitxT", 2), ("y1", 2), ("y2", 2), ("A3", 0), ("A3", 1),
                 ("splitx", 3), ("R", 1, 0), ("R", 1, 1), ("A3", 2), ("R", 1, 2), ("A3", 3),
                 ("R", 1, 3), ("splitxT", 3), ("y1", 3), ("vec", 0), ("y2", 3), ("soft", 0),
                 ("R", 2, 0), ("vec", 1), ("R", 2, 1), ("soft", 1), ("R", 2, 2), ("vec", 2),
                 ("R", 2, 3), ("soft", 2), ("R", 3, 0), ("vecT",), ("R", 3, 1), ("soft", 3),
                 ("wp",), ("R", 3, 2), ("g_bias",), ("R", 3, 3), ("coef",), ("base",)]
        STEADY = [("splitx", 0), ("O1", 0), ("O1", 1), ("splitx", 1), ("y1", 0), ("O1", 2),
                  ("O1", 3), ("y2", 0), ("splitxT", 0), ("y1", 1), ("y2", 1), ("O2", 0),
                  ("splitx", 2), ("O2", 1), ("norm1", 0), ("splitxT", 1), ("O2", 2), ("norm1", 1),
                  ("O2", 3), ("norm1", 2), ("splitx", 3), ("R", 0, 0), ("norm1", 3), ("R", 0, 1),
                  ("T", 0), ("R", 0, 2), ("W", 0, 0), ("R", 0, 3), ("splitxT", 2), ("y1", 2),
                  ("W", 0, 1), ("y2", 2), ("norm2", 0), ("R", 1, 0), ("T", 1), ("scale2", 0),
                  ("R", 1, 1), ("W", 1, 0), ("R", 1, 2), ("W", 1, 1), ("R", 1, 3), ("norm2", 1),
                  ("splitxT", 3), ("y1", 3), ("scale2", 1), ("T", 2), ("y2", 3), ("W", 2, 0),
                  ("R", 2, 0), ("W", 2, 1), ("R", 2, 1), ("norm2", 2), ("R", 2, 2), ("scale2", 2),
                  ("T", 3), ("R", 2, 3), ("W", 3, 0), ("R", 3, 0), ("R", 3, 1), ("R", 3, 2),
                  ("R", 3, 3), ("W", 3, 1), ("norm2", 3), ("base",), ("scale2", 3)]
        LAST = [("O1", 0), ("O1", 1), ("O1", 2), ("O1", 3), ("O2", 0), ("O2", 1), ("norm1", 0),
                ("T", 0), ("O2", 2), ("norm1", 1), ("W", 0, 0), ("O2", 3), ("norm1", 2), ("W", 0, 1),
                ("T", 1), ("norm2", 0), ("norm1", 3), ("W", 1, 0), ("scale2", 0), ("W", 1, 1),
                ("T", 2), ("norm2", 1), ("W", 2, 0), ("scale2", 1), ("W", 2, 1), ("T", 3),
                ("norm2", 2), ("W", 3, 0), ("scale2", 2), ("W", 3, 1), ("norm2", 3), ("scale2", 3)]
        LEFT = ("y1", "y2", "O1", "O2")

        def left_uses(order):
            return [s[:2] for s in order if s[0] in LEFT]

        def left_use(stage, g):
            if isinstance(g, int) and g == 0:
                return left_uses(FIRST).index(stage)
            per = len(left_uses(STEADY))
            order = LAST if isinstance(g, int) and g == G else STEADY
            return per * g + (left_uses(FIRST).__len__() - per + left_uses(order).index(stage))

        def left_bank(stage, g):
            order = FIRST if isinstance(g, int) and g == 0 else \
                LAST if isinstance(g, int) and g == G else STEADY
            return left[left_uses(order).index(stage) % 2]

        def three(pe, bank, weights, moving, first, last):
            pe.matmul(bank, weights[0], moving[0], start=first, stop=False)
            pe.matmul(bank, weights[0], moving[1], start=False, stop=False)
            return pe.matmul(bank, weights[1], moving[0], start=False, stop=last)

        def run(engine, stages):
            for stage in FIRST:
                if stage[0] in stages:
                    stages[stage[0]](0, *stage[1:])
            with engine.Fori(1, G) as g:
                for stage in STEADY:
                    if stage[0] in stages:
                        stages[stage[0]](g, *stage[1:])
            for stage in LAST:
                if stage[0] in stages:
                    stages[stage[0]](G, *stage[1:])

        block = ctx.enter_context(nc.Block())
        x_v = x.rearrange("b (p t) d -> p b (t d)", t=NT)
        xT_v = xT.rearrange("b d n -> d b n")
        out_v = out.rearrange("b (p t) d -> p b t d", t=NT)

        @block.sync
        def _(sp):
            def load(g, b):
                n = GB * g + b
                if not (isinstance(g, int) and g == 0):
                    sp.wait_ge(inner_base, NT * GB * g + NT * (b + 1 - GB))
                sp.dma_start(x_in[:, b, :], x_v[:, bass.ds(n, 1), :].squeeze(1)).then_inc(x_loaded[b], 16)
                sp.dma_start(xt_in[:, b, :], xT_v[:, bass.ds(n, 1), :].squeeze(1)).then_inc(xt_loaded[b], 16)

            def store(h, u):
                sp.wait_ge(out_ready, NT * h + u + 1)
                sp.dma_start(out_v[:, bass.ds(GB * h, GB), u, :], outb[:, u % 2, :, :]).then_inc(slot_free[u % 2], 16)

            sp.dma_start(adj_in, adj.rearrange("(p t) m -> p t m", t=NT)).then_inc(adj_loaded, 16)
            for b in range(GB):
                load(0, b)
            for b in range(GB):
                load(1, b)
            with sp.Fori(2, G) as g:
                for b in range(GB):
                    load(g, b)
                    store(g - 2, b)
            for h in (G - 2, G - 1):
                for u in range(NT):
                    store(h, u)
            for i in range(2):
                sp.wait_ge(slot_free[i], 16 * (1 + G * NT // 2))

        @block.scalar
        def _(act):
            for dst, src, loaded in (
                    (alpha_in[:, :], alpha.rearrange("(p t) -> p t", t=NT), alpha_loaded),
                    (dcol[:, 0:1], dvec.rearrange("(p a) -> p a", a=1), d_loaded),
                    (wT_in[:, :], wT, w_loaded),
                    (fcw_in[:, :], fcw, fcw_loaded),
                    (b_in[:, :], bin_.rearrange("(p a) -> p a", a=1), b_loaded),
                    (nv1_in[:, :, :], nv1T.rearrange("r (t p) -> r t p", t=NT), nv_loaded),
                    (nv2_in[:, :], nv2, nv_loaded)):
                act.dma_start(dst, src).then_inc(loaded, 16)
            w_rows = W.rearrange("(m d) e -> d m e", d=D)
            act.dma_start(wp[:, 0:3, :], w_rows[:, 0:3, :]).then_inc(wp_loaded, 16)
            act.dma_start(wp_more[:, :, :], w_rows[:, 3:5, :]).then_inc(wp_loaded, 16)
            act.dma_start(wp[:, 3:5, :], w_rows[:, 5:7, :]).then_inc(wp_loaded, 16)
            act.dma_start(bias_out[:, :, :], bout.rearrange("p (t e) -> p t e", t=2)).then_inc(bout_loaded, 16)
            act.wait_ge(alpha_loaded, 16)
            nc.scalar.activation(esum[:, :, 0], alpha_in[:, :], ACT.Exp, scale=-1.0).then_inc(gate_exp, 1)
            for n, (lo, hi, src) in enumerate(((1, 2, turn[:, 0:D]), (2, 3, turn[:, D:2 * D]),
                                               (3, 5, turn[:, 2 * D:4 * D]), (5, 9, tail[:, :]))):
                act.wait_ge(cp_made, n + 1)
                nc.scalar.activation(CP[:, lo:hi, :].rearrange("p k d -> p (k d)"), src,
                                     ACT.Copy).then_inc(cp_copied, 1)
            act.wait_ge(a_step, 2)
            nc.scalar.activation(As[0][:, :, :], A, ACT.Copy).then_inc(a_high, 1)

            def power_high(k, mt, bank):
                nc.scalar.activation(TA[k - 1][0][:, mt, :], bank, ACT.Copy).then_inc(t_high, 1)

            for mt in range(NT):
                act.wait_ge(at_turned, mt + 1)
                power_high(1, mt, (left + right)[mt][:, :])
            for mt in range(NT):
                act.wait_ge(t_made, mt + 1)
                power_high(2, mt, (left + right)[mt][:, :])
            act.wait_ge(r_level, STEPS + 1)
            nc.scalar.activation(RC[0][:, :, :], RF[:, :, :, :].rearrange("p i j d -> p i (j d)"),
                                 ACT.Copy).then_inc(rc_high, 1)

            def power3(g, mt):
                act.wait_ge(t_made, NT + mt + 1)
                power_high(3, mt, wide[:, mt % 2, :])

            def soft(g, t):
                act.wait_ge(zneg_done, t + 1)
                nc.scalar.activation(prob[:, 0, :], relu[:, :], ACT.Exp, bias=zneg[:, t:t + 1],
                                     accum_out=zsum[:, t:t + 1]).then_inc(z_exp, 1)
                act.wait_ge(zrec_done, t + 1)
                nc.scalar.activation(prob[:, 1, :], prob[:, 0, :], ACT.Copy, scale=zrec[:, t:t + 1],
                                     accum_out=a1[:, t:t + 1]).then_inc(a_done, 1)

            def wp_high(g):
                act.wait_ge(wp_step, 2)
                nc.scalar.activation(WC[0][:, :], wp[:, :, :].rearrange("p m d -> p (m d)"),
                                     ACT.Copy).then_inc(wc_high, 1)

            def split_x(g, b):
                n = GB * g + b
                act.wait_ge(x_loaded[b], 16 * g + 16)
                if not (isinstance(n, int) and n < 2):
                    act.wait_ge(y_made, 2 * n - 2)
                nc.scalar.activation(xs[0][:, b % 2, :, :].rearrange("p t d -> p (t d)"), x_in[:, b, :],
                                     ACT.Copy).then_inc(xs_high, 1)

            def split_xT(g, b):
                n = GB * g + b
                act.wait_ge(xt_loaded[b], 16 * g + 16)
                if not (isinstance(n, int) and n < 2):
                    act.wait_ge(right_made, NT * (n - 1))
                nc.scalar.activation(yT[0][0][:, b % 2, :], xt_in[:, b, :], ACT.Copy).then_inc(xts_high, 1)

            def y_high(i):
                def stage(g, b):
                    act.wait_ge(y_made, 2 * (GB * g + b) + i)
                    nc.scalar.activation(yT[i][0][:, b % 2, :], left_bank((f"y{i}", b), g)[:, :],
                                         ACT.Copy).then_inc(yT_high, 1)
                return stage

            def inner(g, b, t):
                at = NT * (GB * g + b) + t
                act.wait_ge(right_made, at + 1)
                bank = right[t % 2]
                nc.scalar.activation(Z2[0][:, t, b * D:(b + 1) * D], bank[:, 2 * D:3 * D],
                                     ACT.Copy)
                nc.scalar.activation(Z1[:, t, b, :], bank[:, D:2 * D], ACT.Copy).then_inc(inner_mid, 1)

            def outer1(g, t):
                act.wait_ge(left_drained, left_use(("O1", t), g) + 1)
                nc.scalar.activation(U[0][:, t, :], Z1[:, t, :, :].rearrange("p b d -> p (b d)"),
                                     ACT.Copy).then_inc(u_high, 1)

            def outer2(g, u):
                q = NT * (g - 1) + u
                act.wait_ge(ln1_stat, STAT * (q + 1))
                nc.scalar.activation(LN[0]["sd"][:, u % 2, :], LN[0]["ve"][:, u % 2, :],
                                     ACT.Sqrt).then_inc(ln1_root, 1)

            def turned(g, u):
                q = NT * (g - 1) + u
                act.wait_ge(turn_made, q + 1)
                nc.scalar.activation(x2T[0][:, :, :].rearrange("p b d -> p (b d)"), turn[:, :],
                                     ACT.Copy).then_inc(x2T_high, 1)

            def mix(g, u, half):
                if half == 1:
                    q = NT * (g - 1) + u
                    act.wait_ge(ln2_stat, STAT * (q + 1))
                    nc.scalar.activation(LN[1]["sd"][:, u % 2, :], LN[1]["ve"][:, u % 2, :],
                                         ACT.Sqrt).then_inc(ln2_root, 1)

            def scale2(g, u):
                q = NT * (g - 1) + u
                act.wait_ge(ln2_norm, NORM2 * (q + 1))
                act.wait_ge(slot_free[u % 2], 16 * (NT // 2 * (g - 1) + u // 2 + 1))
                for b in range(GB):
                    last = nc.scalar.activation(outb[:, u % 2, b, :], res[:, u % 2, b, :], ACT.Identity,
                                                bias=LN[1]["nb"][:, u % 2, b:b + 1],
                                                scale=LN[1]["r"][:, u % 2, b:b + 1])
                last.then_inc(out_ready, 1)

            run(act, {"A3": power3, "soft": soft, "wp": wp_high, "splitx": split_x, "splitxT": split_xT,
                      "y1": y_high(1), "y2": y_high(2), "R": inner, "O1": outer1, "O2": outer2,
                      "T": turned, "W": mix, "scale2": scale2})

        @block.gpsimd
        def _(pool):
            nc.gpsimd.memset(ident[:, :], 0.0).then_inc(ident_step, 1)
            nc.gpsimd.memset(eps_c[:, :], EPS).then_inc(ident_step, 1)
            pool.wait_ge(ident_step, 2)
            nc.gpsimd.affine_select(out=ident[:, :], in_=ident[:, :], compare_op=ALU.not_equal, fill=1.0,
                                    base=0, pattern=[[-1, P]], channel_multiplier=1).then_inc(ident_step, 1)
            for i in range(2):
                nc.gpsimd.memset(outb[:, i, :, :], 0.0).then_inc(slot_free[i], 16)
            pool.wait_ge(ident_step, 3)
            pool.wait_ge(wp_loaded, 48)
            nc.gpsimd.tensor_tensor(wp[:, 0, :], wp[:, 0, :], ident[:, :], ALU.add).then_inc(wp_step, 1)
            nc.gpsimd.tensor_tensor(wp[:, 1:3, :], wp[:, 1:3, :], wp_more[:, :, :], ALU.add).then_inc(wp_step, 1)

            def wp_low(g):
                pool.wait_ge(wc_high, 1)
                nc.gpsimd.tensor_tensor(WC[1][:, :], wp[:, :, :].rearrange("p m d -> p (m d)"),
                                        f32(WC[0][:, :]), ALU.subtract).then_inc(wc_low, 1)

            def split_x(g, b):
                n = GB * g + b
                pool.wait_ge(xs_high, n + 1)
                nc.gpsimd.tensor_tensor(xs[1][:, b % 2, :, :].rearrange("p t d -> p (t d)"), x_in[:, b, :],
                                        f32(xs[0][:, b % 2, :, :].rearrange("p t d -> p (t d)")),
                                        ALU.subtract).then_inc(xs_low, 1)

            def split_xT(g, b):
                n = GB * g + b
                pool.wait_ge(xts_high, n + 1)
                nc.gpsimd.tensor_tensor(yT[0][1][:, b % 2, :], xt_in[:, b, :], f32(yT[0][0][:, b % 2, :]),
                                        ALU.subtract).then_inc(xts_low, 1)

            def outer1(g, t):
                pool.wait_ge(u_high, NT * (g - 1) + t + 1)
                nc.gpsimd.tensor_tensor(U[1][:, t, :], Z1[:, t, :, :].rearrange("p b d -> p (b d)"),
                                        f32(U[0][:, t, :]), ALU.subtract).then_inc(u_low, 1)

            def base(g):
                if isinstance(g, int):
                    pool.wait_ge(gb_copied, 1)
                pool.wait_ge(inner_base, NT * GB * (g + 1))
                for t in range(NT):
                    nc.gpsimd.tensor_tensor(
                        Z0[:, t, :, :], Z0[:, t, :, :],
                        g_bias[:, t, :].unsqueeze(1).to_broadcast([P, GB, D]), ALU.add).then_inc(base_full, 1)

            run(pool, {"wp": wp_low, "splitx": split_x, "splitxT": split_xT, "O1": outer1, "base": base})

        @block.vector
        def _(dve):
            v = nc.vector
            dve.wait_ge(d_loaded, 16)
            v.tensor_scalar(dcol[:, 1:2], dcol[:, 0:1], 0.0, 1.0, ALU.max, ALU.min).then_inc(d_step, 1)
            dve.wait_ge(d_step, 1)
            dve.wait_ge(w_loaded, 16)
            v.tensor_scalar(wTs[:, :], wT_in[:, :], dcol[:, 1:2], DT, ALU.mult, ALU.mult).then_inc(d_step, 1)
            dve.wait_ge(gate_exp, 1)
            v.tensor_scalar(esum[:, :, 1], esum[:, :, 0], 1.0, None, ALU.add).then_inc(gate_step, 1)
            dve.wait_ge(gate_step, 1)
            v.reciprocal(esum[:, :, 2], esum[:, :, 1]).then_inc(gate_step, 1)
            dve.wait_ge(gate_step, 2)
            v.tensor_scalar(gcol[:, :], esum[:, :, 2], 0.5 * DT, None, ALU.mult).then_inc(gate_step, 1)
            v.tensor_scalar(ccol[:, :], esum[:, :, 2], -0.5 * DT, 1.0 - DT, ALU.mult, ALU.add).then_inc(gate_step, 1)
            dve.wait_ge(gate_step, 4)
            dve.wait_ge(adj_loaded, 16)
            for t in range(NT):
                last = v.tensor_scalar(A[:, t, :].rearrange("p (b a) -> p b a", b=NT),
                                       adj_in[:, t, :].rearrange("p (a b) -> p b a", b=NT),
                                       gcol[:, t:t + 1], None, ALU.mult)
            last.then_inc(a_step, 1)
            dve.wait_ge(a_step, 1)
            dve.wait_ge(ident_step, 3)
            for t in range(NT):
                last = v.scalar_tensor_tensor(A[:, t, t * P:(t + 1) * P], ident[:, :], ccol[:, t:t + 1],
                                              A[:, t, t * P:(t + 1) * P], ALU.mult, ALU.add)
            last.then_inc(a_step, 1)
            v.tensor_scalar(CP[:, 0, :], ident[:, :], 1.0, None, ALU.mult).then_inc(cp_copied, 1)
            v.tensor_scalar(identdt[:, :], ident[:, :], DT, None, ALU.mult).then_inc(r_level, 1)
            dve.wait_ge(a_high, 1)
            v.tensor_tensor(As[1][:, :, :], A, f32(As[0][:, :, :]), ALU.subtract).then_inc(a_low, 1)
            for mt in range(NT):
                dve.wait_ge(t_high, mt + 1)
                v.tensor_tensor(TA[0][1][:, mt, :], (left + right)[mt][:, :], f32(TA[0][0][:, mt, :]),
                                ALU.subtract).then_inc(t_low, 1)

            dve.wait_ge(cp_copied, 5)
            for p in range(1, STEPS):
                dve.wait_ge(r_level, p)
                for k in range(STEPS - p):
                    acc = RF[:, k % I3, k // I3, :]
                    last = v.scalar_tensor_tensor(acc, CP[:, p, :], DT * comb(k + p, k),
                                                  identdt[:, :] if p == 1 else acc, ALU.mult, ALU.add)
                last.then_inc(r_level, 1)
            dve.wait_ge(r_level, STEPS)
            dve.wait_ge(fc_made, 3)
            dve.wait_ge(q_made, 1)
            for k in range(STEPS + 1):
                p = STEPS - k
                acc = RF[:, k % I3, k // I3, :]
                fc = wide[:, p // 4, (p % 4) * D:(p % 4 + 1) * D] if p < STEPS else turn[:, 0:D]
                if k == STEPS:
                    last = v.tensor_copy(acc, fc)
                else:
                    last = v.scalar_tensor_tensor(acc, fc, float(comb(STEPS, k)),
                                                  acc if k < STEPS - 1 else identdt[:, :], ALU.mult, ALU.add)
            last.then_inc(r_level, 1)
            for mt in range(NT):
                dve.wait_ge(t_high, NT + mt + 1)
                v.tensor_tensor(TA[1][1][:, mt, :], (left + right)[mt][:, :], f32(TA[1][0][:, mt, :]),
                                ALU.subtract).then_inc(t_low, 1)
            dve.wait_ge(rc_high, 1)
            v.tensor_tensor(RC[1][:, :, :], RF[:, :, :, :].rearrange("p i j d -> p i (j d)"),
                            f32(RC[0][:, :, :]), ALU.subtract).then_inc(rc_low, 1)

            def vec_split(r):
                dve.wait_ge(v_step, 3 * r + 1)
                v.tensor_copy(Vs[0][:, r, :, :], V[:, :, NV * r:NV * r + NV]).then_inc(v_step, 1)
                dve.wait_ge(v_step, 3 * r + 2)
                v.tensor_tensor(Vs[1][:, r, :, :], V[:, :, NV * r:NV * r + NV], f32(Vs[0][:, r, :, :]),
                                ALU.subtract).then_inc(v_step, 1)

            def power3(g, mt):
                dve.wait_ge(t_high, 2 * NT + mt + 1)
                v.tensor_tensor(TA[2][1][:, mt, :], wide[:, mt % 2, :], f32(TA[2][0][:, mt, :]),
                                ALU.subtract).then_inc(t_low, 1)
                if mt == 0:
                    v.tensor_reduce(s1[:, :], adj_in, AX.X, ALU.add).then_inc(rowsum_done, 1)
                    v.memset(V[:, :, :], 1.0).then_inc(rowsum_done, 1)
                    v.memset(Qc[:, :], 0.0).then_inc(rowsum_done, 1)
                    dve.wait_ge(rowsum_done, 3)
                    v.tensor_tensor(V[:, :, 1], s1[:, :], gcol[:, :], ALU.mult).then_inc(rowsum_done, 1)
                    v.tensor_tensor(s2[:, :], s1[:, :], s1[:, :], ALU.mult)
                    dve.wait_ge(rowsum_done, 4)
                    v.tensor_tensor(V[:, :, 1], V[:, :, 1], ccol[:, :], ALU.add).then_inc(rowsum_done, 1)
                    dve.wait_ge(rowsum_done, 5)
                    v.tensor_copy(Vs[0][:, 1, :, :], V[:, :, 0:NV]).then_inc(rowsum_done, 1)
                    dve.wait_ge(rowsum_done, 6)
                    v.tensor_tensor(Vs[1][:, 1, :, :], V[:, :, 0:NV], f32(Vs[0][:, 1, :, :]),
                                    ALU.subtract).then_inc(rowsum_done, 1)
                    dve.wait_ge(q_made, 1)
                    for k in range(STEPS + 1):
                        src = turn[:, D + STEPS - k:D + STEPS - k + 1]
                        last = v.tensor_scalar(Qc[:, k + k // I3:k + k // I3 + 1], src,
                                               float(comb(STEPS, k)), None, ALU.mult)
                    last.then_inc(q_scaled, 1)

            def vec(g, r):
                dve.wait_ge(v_made, r + 1)
                made = turn[:, 256 + 64 * r:256 + 64 * r + NT * NV].rearrange("p (t c) -> p t c", t=NT)
                if r == 0:
                    v.tensor_copy(V[:, :, 2], made[:, :, 1]).then_inc(v_step, 1)
                else:
                    v.tensor_copy(V[:, :, NV * r:NV * r + NV], made).then_inc(v_step, 1)
                if r < 2:
                    vec_split(r)

            def vecT(g):
                dve.wait_ge(q_turned, 1)
                v.tensor_copy(Q12[:, :], turn[0:I3 * NV, 0:D]).then_inc(q_copied, 1)
                dve.wait_ge(v_turned, 1)
                v.tensor_copy(V12[:, :, :].rearrange("k t p -> k (t p)"), wide[0:I3 * NV, 0, :]).then_inc(v_copied, 1)

            def bias_part(g):
                dve.wait_ge(gb_made, 1)
                v.tensor_copy(g_bias[:, :, :].rearrange("p t d -> p (t d)"), wide[:, 1, :]).then_inc(gb_copied, 1)

            def soft(g, t):
                dve.wait_ge(z_made, t + 1)
                if t >= 1:
                    dve.wait_ge(z_exp, t)
                v.tensor_scalar(relu[:, :], tail[:, :], 0.0, None, ALU.max).then_inc(relu_done, 1)
                dve.wait_ge(relu_done, t + 1)
                v.tensor_reduce(zmax[:, t:t + 1], relu[:, :], AX.X, ALU.max).then_inc(a_step, 1)
                dve.wait_ge(a_step, 2 + t + 1)
                v.tensor_scalar(zneg[:, t:t + 1], zmax[:, t:t + 1], -1.0, None, ALU.mult).then_inc(zneg_done, 1)
                dve.wait_ge(z_exp, t + 1)
                v.reciprocal(zrec[:, t:t + 1], zsum[:, t:t + 1]).then_inc(zrec_done, 1)

            def coef(g):
                dve.wait_ge(a_done, NT)
                v.tensor_tensor(a2[:, :], a1[:, :], a1[:, :], ALU.mult).then_inc(coef_done, 1)

            def y_low(i):
                def stage(g, b):
                    dve.wait_ge(yT_high, 2 * (GB * g + b) + i)
                    v.tensor_tensor(yT[i][1][:, b % 2, :], left_bank((f"y{i}", b), g)[:, :],
                                    f32(yT[i][0][:, b % 2, :]), ALU.subtract).then_inc(left_drained, 1)
                return stage

            def inner(g, b, t):
                at = NT * (GB * g + b) + t
                bank = right[t % 2]
                dve.wait_ge(inner_mid, at + 1)
                v.tensor_tensor(Z0[:, t, b, :], bank[:, 0:D], x_in[:, b, t * D:(t + 1) * D],
                                ALU.add).then_inc(inner_base, 1)
                v.tensor_tensor(Z2[1][:, t, b * D:(b + 1) * D], bank[:, 2 * D:3 * D],
                                f32(Z2[0][:, t, b * D:(b + 1) * D]), ALU.subtract).then_inc(inner_low, 1)

            def outer1(g, t):
                dve.wait_ge(o1_made, NT * (g - 1) + t + 1)
                dve.wait_ge(inner_mid, NT * GB * g)
                z1 = Z1[:, t, :, :].rearrange("p b d -> p (b d)")
                v.tensor_tensor(z1, left_bank(("O1", t), g)[:, :], z1, ALU.add).then_inc(left_drained, 1)

            def stats(ln, src, u, step, at):
                for b in range(GB):
                    last = v.bn_stats(ln["st"][:, u % 2, b, :], src[:, b, :])
                last.then_inc(step, 1)
                dve.wait_ge(step, at + 1)
                s, st = u % 2, ln["st"][:, u % 2, :, :]
                v.tensor_tensor(ln["msum"][:, s, :], st[:, :, 1], st[:, :, 4], ALU.add)
                v.tensor_tensor(ln["mdif"][:, s, :], st[:, :, 1], st[:, :, 4], ALU.subtract)
                v.tensor_tensor(ln["m2"][:, s, :], st[:, :, 2], st[:, :, 5], ALU.add).then_inc(step, 1)
                dve.wait_ge(step, at + 2)
                v.tensor_scalar(ln["mean"][:, s, :], ln["msum"][:, s, :], 0.5, None, ALU.mult)
                v.tensor_scalar(ln["within"][:, s, :], ln["m2"][:, s, :], 1.0 / D, EPS, ALU.mult, ALU.add)
                v.scalar_tensor_tensor(ln["between"][:, s, :], ln["mdif"][:, s, :], 0.25, ln["mdif"][:, s, :],
                                       ALU.mult, ALU.mult).then_inc(step, 1)
                dve.wait_ge(step, at + 3)
                v.tensor_tensor(ln["ve"][:, s, :], ln["within"][:, s, :], ln["between"][:, s, :],
                                ALU.add).then_inc(step, 1)

            def rsqrt(ln, u, step, at):
                s = u % 2
                v.reciprocal(ln["r0"][:, s, :], ln["sd"][:, s, :]).then_inc(step, 1)
                dve.wait_ge(step, at + 1)
                v.tensor_tensor(ln["q"][:, s, :], ln["r0"][:, s, :], ln["r0"][:, s, :], ALU.mult).then_inc(step, 1)
                dve.wait_ge(step, at + 2)
                v.scalar_tensor_tensor(ln["q2"][:, s, :], ln["q"][:, s, :], -0.5, ln["ve"][:, s, :],
                                       ALU.mult, ALU.mult).then_inc(step, 1)
                dve.wait_ge(step, at + 3)
                v.scalar_tensor_tensor(ln["r"][:, s, :], ln["q2"][:, s, :], 1.5, ln["r0"][:, s, :],
                                       ALU.add, ALU.mult).then_inc(step, 1)
                dve.wait_ge(step, at + 4)

            def outer2(g, u):
                q = NT * (g - 1) + u
                dve.wait_ge(o2_made, q + 1)
                dve.wait_ge(base_full, q + 1)
                v.tensor_tensor(x2[:, u, :, :].rearrange("p b d -> p (b d)"), left_bank(("O2", u), g)[:, :],
                                Z0[:, u, :, :].rearrange("p b d -> p (b d)"), ALU.add).then_inc(left_drained, 1)
                dve.wait_ge(left_drained, left_use(("O2", u), g) + 1)
                stats(LN[0], x2[:, u, :, :], u, ln1_stat, STAT * q)

            def norm1(g, u):
                q = NT * (g - 1) + u
                dve.wait_ge(ln1_root, q + 1)
                rsqrt(LN[0], u, ln1_norm, NORM1 * q)
                for b in range(GB):
                    last = v.tensor_scalar(x2[:, u, b, :], x2[:, u, b, :], LN[0]["mean"][:, u % 2, b:b + 1],
                                           LN[0]["r"][:, u % 2, b:b + 1], ALU.subtract, ALU.mult)
                last.then_inc(x2_ready, 1)

            def turned(g, u):
                dve.wait_ge(x2T_high, NT * (g - 1) + u + 1)
                v.tensor_tensor(x2T[1][:, :, :].rearrange("p b d -> p (b d)"), turn[:, :],
                                f32(x2T[0][:, :, :].rearrange("p b d -> p (b d)")),
                                ALU.subtract).then_inc(x2T_low, 1)

            def mix(g, u, half):
                at = 2 * (NT * (g - 1) + u) + half
                r = res[:, u % 2, 2 * half:2 * half + 2, :]
                dve.wait_ge(wide_made, at + 1)
                v.tensor_tensor(r, wide[:, :, 0:D], bias_out[:, :, :], ALU.add).then_inc(mixed, 1)
                for n, (part, factor) in enumerate(((wide[:, :, D:2 * D], s1), (wide[:, :, 2 * D:3 * D], s2),
                                                    (tail_v[:, :, 0:D], a1), (tail_v[:, :, D:2 * D], a2))):
                    dve.wait_ge(mixed, MIX * at + n + 1)
                    v.scalar_tensor_tensor(r, part, factor[:, u:u + 1], r, ALU.mult, ALU.add).then_inc(mixed, 1)
                if half == 1:
                    dve.wait_ge(mixed, MIX * (at + 1))
                    stats(LN[1], res[:, u % 2, :, :], u, ln2_stat, STAT * (NT * (g - 1) + u))

            def norm2(g, u):
                q = NT * (g - 1) + u
                dve.wait_ge(ln2_root, q + 1)
                rsqrt(LN[1], u, ln2_norm, NORM2 * q)
                v.scalar_tensor_tensor(LN[1]["nb"][:, u % 2, :], LN[1]["mean"][:, u % 2, :], -1.0,
                                       LN[1]["r"][:, u % 2, :], ALU.mult, ALU.mult).then_inc(ln2_norm, 1)

            dve.wait_ge(bout_loaded, 16)
            run(dve, {"A3": power3, "vec": vec, "vecT": vecT, "g_bias": bias_part, "soft": soft,
                      "coef": coef, "y1": y_low(1), "y2": y_low(2), "R": inner, "O1": outer1,
                      "O2": outer2, "norm1": norm1, "T": turned, "W": mix, "norm2": norm2})

        @block.tensor
        def _(pe):
            pe.wait_ge(d_step, 2)
            pe.matmul(turn[:, 0:D], wTs[:, :], wT_in[:, :], start=True, stop=True).then_inc(cp_made, 1)
            pe.wait_ge(cp_copied, 2)
            pe.matmul(turn[:, D:2 * D], CP[:, 1, :], CP[:, 1, :], start=True, stop=True).then_inc(cp_made, 1)
            pe.wait_ge(cp_copied, 3)
            pe.matmul(turn[:, 2 * D:4 * D], CP[:, 2, :], CP[:, 1:3, :].rearrange("p k d -> p (k d)"),
                      start=True, stop=True).then_inc(cp_made, 1)
            pe.wait_ge(cp_copied, 4)
            pe.matmul(tail[:, :], CP[:, 4, :], CP[:, 1:5, :].rearrange("p k d -> p (k d)"),
                      start=True, stop=True).then_inc(cp_made, 1)
            pe.wait_ge(a_step, 2)
            for mt in range(NT):
                for t in range(NT):
                    last = pe.transpose((left + right)[mt][:, t * P:(t + 1) * P],
                                        A[:, t, mt * P:(mt + 1) * P], ident[:, :])
                last.then_inc(at_turned, 1)
            pe.wait_ge(cp_copied, 5)
            pe.wait_ge(fcw_loaded, 16)
            for lo, hi, bank in ((0, 4, wide[:, 0, :]), (4, 8, wide[:, 1, :]), (8, 9, turn[:, 0:D])):
                pe.matmul(bank, fcw_in[:, :], CP[:, lo:hi, :].rearrange("p k d -> p (k d)"),
                          start=True, stop=True).then_inc(fc_made, 1)
            pe.wait_ge(b_loaded, 16)
            for p in range(STEPS + 1):
                last = pe.matmul(turn[:, D + p:D + p + 1], CP[:, p, :], b_in[:, :], start=True, stop=True)
            last.then_inc(q_made, 1)

            def power(k, mt, bank):
                for kt in range(NT):
                    last = three(pe, bank, [a[:, kt, mt * P:(mt + 1) * P] for a in As],
                                 [a[:, kt, :] for a in TA[k - 2]], kt == 0, kt == NT - 1)
                last.then_inc(t_made, 1)

            pe.wait_ge(a_low, 1)
            pe.wait_ge(t_low, NT)
            for mt in range(NT):
                power(2, mt, (left + right)[mt][:, :])

            def power3(g, mt):
                if mt == 0:
                    pe.wait_ge(t_low, 2 * NT)
                    pe.wait_ge(rc_high, 1)
                if mt >= 2:
                    pe.wait_ge(t_low, 2 * NT + mt - 1)
                power(3, mt, wide[:, mt % 2, :])

            def vec(g, r):
                if r == 0:
                    pe.wait_ge(rowsum_done, 7)
                    pe.wait_ge(q_scaled, 1)
                else:
                    pe.wait_ge(v_step, 3 * r)
                src, cols, mats = (1, 2, TA[0]) if r == 0 else (r - 1, NV, TA[2])
                if r == 1:
                    pe.wait_ge(t_low, 3 * NT)
                for t in range(NT):
                    o = 256 + 64 * r + NV * t
                    for kt in range(NT):
                        last = three(pe, turn[:, o:o + cols], [a[:, kt, t * P:(t + 1) * P] for a in mats],
                                     [a[:, src, kt, 0:cols] for a in Vs], kt == 0, kt == NT - 1)
                last.then_inc(v_made, 1)

            def vecT(g):
                pe.wait_ge(v_step, 7)
                pe.transpose(turn[0:I3 * NV, 0:D], Qc[:, :], ident[:, :]).then_inc(q_turned, 1)
                for t in range(NT):
                    last = pe.transpose(wide[0:I3 * NV, 0, t * P:(t + 1) * P], V[:, t, :], ident[:, :])
                last.then_inc(v_turned, 1)

            def bias_part(g):
                pe.wait_ge(q_copied, 1)
                pe.wait_ge(v_copied, 1)
                for t in range(NT):
                    last = pe.matmul(wide[:, 1, t * D:(t + 1) * D], V12[:, t, :], Q12[:, :], start=True, stop=True)
                last.then_inc(gb_made, 1)

            def soft(g, t):
                if t == 0:
                    pe.wait_ge(nv_loaded, 32)
                else:
                    pe.wait_ge(relu_done, t)
                pe.matmul(tail[:, :], nv1_in[:, t, :], nv2_in[:, :], start=True, stop=True).then_inc(z_made, 1)

            def left_free(stage, g):
                use = left_use(stage, g)
                if isinstance(use, int) and use < 2:
                    return
                pe.wait_ge(left_drained, use - 1)

            def y(i):
                def stage(g, b):
                    pe.wait_ge(xs_low, GB * g + b + 1)
                    if isinstance(g, int) and b == 0:
                        pe.wait_ge(t_low, NT + 1 if i == 1 else 2 * NT)
                    left_free((f"y{i}", b), g)
                    for kt in range(NT):
                        last = three(pe, left_bank((f"y{i}", b), g)[:, :], [a[:, b % 2, kt, :] for a in xs],
                                     [a[:, kt, :] for a in TA[i - 1]], kt == 0, kt == NT - 1)
                    last.then_inc(y_made, 1)
                return stage

            def inner(g, b, t):
                at = NT * (GB * g + b) + t
                if t == 0:
                    pe.wait_ge(xts_low, GB * g + b + 1)
                    pe.wait_ge(left_drained, left_use(("y2", b), g) + 1)
                if isinstance(g, int) and b == 0 and t == 0:
                    pe.wait_ge(rc_low, 1)
                if not (isinstance(at, int) and at < 2):
                    pe.wait_ge(inner_low, at - 1)
                for i in range(I3):
                    last = three(pe, right[t % 2][:, 0:J3 * D], [a[:, b % 2, t * P:(t + 1) * P] for a in yT[i]],
                                 [a[:, i, :] for a in RC], i == 0, i == I3 - 1)
                last.then_inc(right_made, 1)

            def outer(moving, made, name):
                def stage(g, t):
                    if name == "O1":
                        pe.wait_ge(inner_low, NT * GB * g)
                    else:
                        pe.wait_ge(u_low, NT * g)
                    left_free((name, t), g)
                    for kt in range(NT):
                        last = three(pe, left_bank((name, t), g)[:, :],
                                     [a[:, kt, t * P:(t + 1) * P] for a in TA[2]],
                                     [a[:, kt, :] for a in moving], kt == 0, kt == NT - 1)
                    last.then_inc(made, 1)
                return stage

            def turned(g, u):
                q = NT * (g - 1) + u
                pe.wait_ge(x2_ready, q + 1)
                for b in range(GB):
                    last = pe.transpose(turn[:, b * P:(b + 1) * P], x2[:, u, b, :], ident[:, :])
                last.then_inc(turn_made, 1)

            def mix(g, u, half):
                q = NT * (g - 1) + u
                pe.wait_ge(x2T_low, q + 1)
                if u or half:
                    pe.wait_ge(mixed, MIX * (2 * q + half))
                if u == 0 and half == 0:
                    pe.wait_ge(wc_low, 1)
                for t in range(2):
                    weights = [a[:, 2 * half + t, :] for a in x2T]
                    three(pe, wide[:, t, 0:PW], weights, [a[:, 0:PW] for a in WC], True, True)
                    last = three(pe, tail_v[:, t, :], weights, [a[:, PW:NP5 * D] for a in WC], True, True)
                last.then_inc(wide_made, 1)

            run(pe, {"A3": power3, "vec": vec, "vecT": vecT, "g_bias": bias_part, "soft": soft,
                     "y1": y(1), "y2": y(2), "R": inner, "O1": outer(Z2, o1_made, "O1"),
                     "O2": outer(U, o2_made, "O2"), "T": turned, "W": mix})


def kernel(x, adj, L0_gnn_alpha_train, L0_gnn_w, L0_gnn_d, L0_gnn_fc_in_w, L0_gnn_fc_in_b,
           L1_gnn_node_vec1, L1_gnn_node_vec2, L1_gnn_W, L1_gnn_b):
    import numpy as np
    import concourse.bacc as bacc
    from concourse.bass_utils import run_bass_kernel_spmd

    B, N, D = x.shape
    T = 4
    x, nv1 = np.asarray(x), np.asarray(L1_gnn_node_vec1)
    arrays = {
        "x": x,
        "xT": x.reshape(B, N // T, T, D).transpose(0, 3, 2, 1).reshape(B, D, N),
        "adj": adj,
        "alpha": L0_gnn_alpha_train,
        "wT": np.asarray(L0_gnn_w).T,
        "dvec": L0_gnn_d,
        "fcw": L0_gnn_fc_in_w,
        "bin": L0_gnn_fc_in_b,
        "nv1T": nv1.reshape(N // T, T, nv1.shape[1]).transpose(2, 1, 0).reshape(nv1.shape[1], N),
        "nv2": L1_gnn_node_vec2,
        "W": L1_gnn_W,
        "bout": np.broadcast_to(np.asarray(L1_gnn_b), (128, 2, D)).reshape(128, 2 * D),
    }
    nc = bacc.Bacc("TRN2", target_bir_lowering=False, num_devices=1)
    feeds, args = {}, []
    for name, a in arrays.items():
        a = np.ascontiguousarray(a)
        feeds[f"in_{name}"] = a
        args.append(nc.dram_tensor(f"in_{name}", a.shape, mybir.dt.from_np(a.dtype), kind="ExternalInput").ap())
    args.append(nc.dram_tensor("out", (B, N, D), mybir.dt.float32, kind="ExternalOutput").ap())
    graph_resnorm_kernel(nc, *args)
    r = run_bass_kernel_spmd(nc, [feeds], core_ids=[0])
    return r.results[0]["out"]
```

```python
import concourse.bass as bass
from concourse import mybir
from contextlib import ExitStack
from math import comb


def graph_resnorm_kernel(nc, x, xT, adj, alpha, wT, dvec, fcw, bin_, nv1T, nv2, W, bout, out):
    F32 = mybir.dt.float32
    F32R = mybir.dt.float32r
    ALU = mybir.AluOpType
    ACT = mybir.ActivationFunctionType
    AX = mybir.AxisListType

    P = nc.NUM_PARTITIONS
    B, N, D = x.shape
    NT = N // P
    GB = 4
    G = B // GB
    RANK = nv1T.shape[0]
    STEPS = 8
    DT = 1.0 / STEPS
    EPS = 1e-5
    I3 = J3 = 3
    NP5 = 5
    PW = 3 * D
    NV = 4
    VROW = (3, 1, 2)

    ctx = ExitStack()
    with ctx:
        def sb(name, shape, dt=F32):
            return ctx.enter_context(nc.sbuf_tensor(name, shape, dt))

        def pb(name, shape, dt=F32):
            return ctx.enter_context(nc.psum_tensor(name, shape, dt))

        def sem(name):
            return ctx.enter_context(nc.semaphore(name))

        def f32(ap):
            return ap.bitcast(F32)

        ident = sb("ident", [P, P])
        identdt = sb("identdt", [P, P])
        TA = [[sb(f"A{k}T_{part}", [P, NT, N], F32R) for part in ("hi", "lo")] for k in (1, 2, 3)]
        RC = [sb(f"R_{part}", [P, I3, J3 * D], F32R) for part in ("hi", "lo")]
        WC = [sb(f"WP_{part}", [P, NP5 * D], F32R) for part in ("hi", "lo")]
        wp = sb("wp", [P, NP5, D])
        wp_more = sb("wp_more", [P, 2, D])
        bias_out = sb("bias_out", [P, 2, D])
        g_bias = sb("g_bias", [P, NT, D])
        s1 = sb("s1", [P, NT])
        s2 = sb("s2", [P, NT])
        a1 = sb("a1", [P, NT])
        a2 = sb("a2", [P, NT])
        eps_c = sb("eps_c", [P, 1])
        x_in = sb("x_in", [P, GB, NT * D])
        xt_in = sb("xt_in", [P, GB, N])
        xs = [sb(f"x_{part}", [P, 2, NT, D], F32R) for part in ("hi", "lo")]
        yT = [[sb(f"y{i}T_{part}", [P, 2, N], F32R) for part in ("hi", "lo")] for i in range(I3)]
        Z0 = sb("Z0", [P, NT, GB, D])
        Z1 = sb("Z1", [P, NT, GB, D])
        Z2 = [sb(f"Z2_{part}", [P, NT, GB * D], F32R) for part in ("hi", "lo")]
        U = [sb(f"U_{part}", [P, NT, GB * D], F32R) for part in ("hi", "lo")]
        x2 = sb("x2", [P, NT, GB, D])
        x2T = [sb(f"x2T_{part}", [P, 2, GB, D], F32R) for part in ("hi", "lo")]
        res = sb("res", [P, 2, GB, D])
        adapt = sb("adapt", [P, 2, 2, D])
        outb = sb("outb", [P, 2, GB, D])
        LN = [dict({"st": sb(f"st{l}", [P, 2, GB, 6]), "mv": sb(f"mv{l}", [P, 2, GB, 2])},
                   **{name: sb(f"{name}{l}", [P, 2, GB]) for name in ("sd", "r0", "q", "q2", "r", "nb")})
              for l in (1, 2)]
        alpha_in = sb("alpha_in", [P, NT])
        esum = sb("esum", [P, NT, 4])
        gcol = sb("gcol", [P, NT])
        ccol = sb("ccol", [P, NT])
        dcol = sb("dcol", [P, 2])
        wT_in = sb("wT_in", [P, D])
        wTs = sb("wTs", [P, D])
        fcw_in = sb("fcw_in", [P, D])
        b_in = sb("b_in", [P, 1])
        RF = sb("RF", [P, I3, J3, D])
        Qc = sb("Qc", [P, I3 * NV])
        Qrow = sb("Qrow", [NV, I3, D])
        V = sb("V", [P, NT, I3 * NV])
        Vs = [sb(f"V_{part}", [P, I3, NT, NV], F32R) for part in ("hi", "lo")]
        nv1_in = sb("nv1_in", [RANK, NT, P])
        nv2_in = sb("nv2_in", [RANK, N])
        zmax = sb("zmax", [P, NT])
        zneg = sb("zneg", [P, NT])
        zsum = sb("zsum", [P, NT])
        zrec = sb("zrec", [P, NT])
        prob = res[:, :, :, :].rearrange("p s b d -> p s (b d)")
        adj_in = x2[:, :, :, :].rearrange("p t b d -> p t (b d)")
        A = Z0[:, :, :, :].rearrange("p t b d -> p t (b d)")
        As = U
        Vrow = adj_in[0:NV, :, :]
        CP = Z1[:, :, :, :].rearrange("p t b d -> p (t b) d")[:, 0:STEPS + 1, :]
        relu = outb[:, 0, :, :].rearrange("p b d -> p (b d)")

        left = [pb(f"left{i}", [P, 512]) for i in range(2)]
        right = [pb(f"right{i}", [P, 512]) for i in range(2)]
        turn = pb("turn", [P, 512])
        wide = pb("wide", [P, 2, 512])
        tail = pb("tail", [P, 512])
        A2_BANKS = [right[0][:, :], right[1][:, :], wide[:, 0, :], wide[:, 1, :]]
        tail_v = tail[:, :].rearrange("p (t c) -> p t c", t=2)

        adj_loaded = [sem(f"adj_loaded{t}") for t in range(NT)]
        w_loaded, d_loaded, fcw_loaded, b_loaded = map(
            sem, ("w_loaded", "d_loaded", "fcw_loaded", "b_loaded"))
        alpha_loaded, nv_loaded, wp_loaded, bout_loaded = map(
            sem, ("alpha_loaded", "nv_loaded", "wp_loaded", "bout_loaded"))
        ident_step, gate_exp, gate_step, d_step, a_step = map(
            sem, ("ident_step", "gate_exp", "gate_step", "d_step", "a_step"))
        a_high, a_low, at_turned, t_high, t_low, t_made = map(
            sem, ("a_high", "a_low", "at_turned", "t_high", "t_low", "t_made"))
        cp_made, cp_copied, fc_made, r_level, rc_high, rc_low = map(
            sem, ("cp_made", "cp_copied", "fc_made", "r_level", "rc_high", "rc_low"))
        q_made, q_scaled, q_turned, q_copied = map(sem, ("q_made", "q_scaled", "q_turned", "q_copied"))
        v_step, v_made, v_rows, v_back, v_turned, v_copied, gb_made, gb_copied = map(
            sem, ("v_step", "v_made", "v_rows", "v_back", "v_turned", "v_copied", "gb_made", "gb_copied"))
        wp_step, wc_high, wc_low = map(sem, ("wp_step", "wc_high", "wc_low"))
        z_made, relu_done, zneg_done, z_exp, zrec_done, a_done, coef_done = map(
            sem, ("z_made", "relu_done", "zneg_done", "z_exp", "zrec_done", "a_done", "coef_done"))
        rowsum_done = sem("rowsum_done")
        x_loaded = [sem(f"x_loaded{i}") for i in range(GB)]
        xt_loaded = [sem(f"xt_loaded{i}") for i in range(GB)]
        xs_high, xs_low, xts_high, xts_low = map(sem, ("xs_high", "xs_low", "xts_high", "xts_low"))
        y_made, o1_made, o2_made, left_drained, yT_high = map(
            sem, ("y_made", "o1_made", "o2_made", "left_drained", "yT_high"))
        right_made, inner_mid, inner_base, inner_low = map(
            sem, ("right_made", "inner_mid", "inner_base", "inner_low"))
        u_high, u_low, base_full = map(sem, ("u_high", "u_low", "base_full"))
        ln1_stat, ln1_root, ln1_norm, x2_ready, turn_made, x2T_high, x2T_low = map(
            sem, ("ln1_stat", "ln1_root", "ln1_norm", "x2_ready", "turn_made", "x2T_high", "x2T_low"))
        wide_made, mixed, tail_taken, adapt_sum, res_full, ln2_stat, ln2_root, ln2_norm, out_ready = map(
            sem, ("wide_made", "mixed", "tail_taken", "adapt_sum", "res_full", "ln2_stat", "ln2_root", "ln2_norm", "out_ready"))
        stats_seen = sem("stats_seen")
        slot_free = [sem(f"slot_free{i}") for i in range(2)]
        MIX = 3
        STAT = 2
        NORM = 5

        FIRST = [("splitx", 0), ("AT",), ("C34",), ("A",), ("y1", 0), ("A2", 0), ("C58",),
                 ("A2", 1), ("Rsum",), ("splitx", 1), ("splitxT", 0), ("A2", 2), ("A2", 3),
                 ("y1", 1), ("FC",), ("RC",), ("y2", 0), ("splitxT", 1), ("y2", 1), ("splitx", 2),
                 ("R", 0, 0), ("R", 0, 1), ("R", 0, 2), ("R", 0, 3), ("splitxT", 2), ("y1", 2),
                 ("splitx", 3), ("y2", 2), ("A3", 0), ("A3", 1), ("R", 1, 0), ("R", 1, 1),
                 ("A3", 2), ("R", 1, 2), ("A3", 3), ("R", 1, 3), ("splitxT", 3), ("y1", 3),
                 ("vec", 0), ("y2", 3), ("vback", 0), ("soft", 0), ("R", 2, 0), ("vec", 1),
                 ("R", 2, 1), ("vback", 1), ("soft", 1), ("R", 2, 2), ("vec", 2), ("R", 2, 3),
                 ("soft", 2), ("wp",), ("R", 3, 0), ("vecT",), ("soft", 3), ("R", 3, 1),
                 ("gbias",), ("R", 3, 2), ("base", 0), ("coef",), ("R", 3, 3), ("base", 1),
                 ("base", 2), ("base", 3)]
        STEADY = [("splitx", 0), ("O1", 0), ("O1", 1), ("O1", 2), ("O1", 3), ("splitxT", 0),
                  ("y1", 0), ("O2", 0), ("stat1", 0), ("O2", 1), ("splitx", 1), ("stat1", 1),
                  ("norm1", 0), ("y2", 0), ("O2", 2), ("scale1", 0), ("T", 0), ("norm1", 1),
                  ("R", 0, 0), ("stat1", 2), ("splitx", 2), ("R", 0, 1), ("norm1", 2), ("W", 0, 0),
                  ("splitxT", 1), ("O2", 3), ("y1", 1), ("scale1", 1), ("W", 0, 1), ("scale1", 2),
                  ("y2", 1), ("T", 1), ("R", 0, 2), ("R", 0, 3), ("R", 1, 0), ("splitxT", 2),
                  ("stat2", 0), ("W", 1, 0), ("stat1", 3), ("R", 1, 1), ("R", 1, 2), ("norm2", 0),
                  ("norm1", 3), ("W", 1, 1), ("scale2", 0), ("y1", 2), ("T", 2), ("R", 1, 3),
                  ("scale1", 3), ("stat2", 1), ("splitx", 3), ("norm2", 1), ("y2", 2), ("W", 2, 0),
                  ("T", 3), ("R", 2, 0), ("y1", 3), ("splitxT", 3), ("y2", 3), ("scale2", 1),
                  ("W", 2, 1), ("R", 2, 1), ("stat2", 2), ("R", 2, 2), ("R", 2, 3), ("W", 3, 0),
                  ("R", 3, 0), ("R", 3, 1), ("norm2", 2), ("R", 3, 2), ("base", 0), ("W", 3, 1),
                  ("R", 3, 3), ("base", 1), ("stat2", 3), ("norm2", 3), ("base", 2), ("scale2", 2),
                  ("scale2", 3), ("base", 3)]
        LAST = [("O1", 0), ("O1", 1), ("O1", 2), ("O1", 3), ("O2", 0), ("stat1", 0), ("norm1", 0),
                ("scale1", 0), ("O2", 1), ("stat1", 1), ("O2", 2), ("norm1", 1), ("T", 0),
                ("scale1", 1), ("stat1", 2), ("O2", 3), ("W", 0, 0), ("norm1", 2), ("T", 1),
                ("W", 0, 1), ("scale1", 2), ("stat1", 3), ("stat2", 0), ("W", 1, 0), ("norm2", 0),
                ("T", 2), ("W", 1, 1), ("scale2", 0), ("norm1", 3), ("scale1", 3), ("stat2", 1),
                ("W", 2, 0), ("norm2", 1), ("T", 3), ("W", 2, 1), ("scale2", 1), ("W", 3, 0),
                ("stat2", 2), ("W", 3, 1), ("norm2", 2), ("scale2", 2), ("stat2", 3), ("norm2", 3),
                ("scale2", 3)]
        LEFT = ("y1", "y2", "O1", "O2")

        def left_uses(order):
            return [s[:2] for s in order if s[0] in LEFT]

        def left_use(stage, g):
            if isinstance(g, int) and g == 0:
                return left_uses(FIRST).index(stage)
            per = len(left_uses(STEADY))
            order = LAST if isinstance(g, int) and g == G else STEADY
            return per * g + (left_uses(FIRST).__len__() - per + left_uses(order).index(stage))

        def left_bank(stage, g):
            order = FIRST if isinstance(g, int) and g == 0 else \
                LAST if isinstance(g, int) and g == G else STEADY
            return left[left_uses(order).index(stage) % 2]

        def y_use(i, b, g):
            order = FIRST if isinstance(g, int) and g == 0 else STEADY
            ys = [s for s in order if s[0] in ("y1", "y2")]
            return len(ys) * g + ys.index((f"y{i}", b))

        def three(pe, bank, weights, moving, first, last):
            pe.matmul(bank, weights[0], moving[0], start=first, stop=False)
            pe.matmul(bank, weights[0], moving[1], start=False, stop=False)
            return pe.matmul(bank, weights[1], moving[0], start=False, stop=last)

        def run(engine, stages):
            for stage in FIRST:
                if stage[0] in stages:
                    stages[stage[0]](0, *stage[1:])
            with engine.Fori(1, G) as g:
                for stage in STEADY:
                    if stage[0] in stages:
                        stages[stage[0]](g, *stage[1:])
            for stage in LAST:
                if stage[0] in stages:
                    stages[stage[0]](G, *stage[1:])

        block = ctx.enter_context(nc.Block())
        x_v = x.rearrange("b (p t) d -> p b (t d)", t=NT)
        xT_v = xT.rearrange("b d n -> d b n")
        out_v = out.rearrange("b (p t) d -> p b t d", t=NT)

        @block.sync
        def _(sp):
            def load(g, b):
                n = GB * g + b
                if not (isinstance(g, int) and g == 0):
                    sp.wait_ge(inner_base, NT * GB * g + NT * (b + 1 - GB))
                sp.dma_start(x_in[:, b, :], x_v[:, bass.ds(n, 1), :].squeeze(1)).then_inc(x_loaded[b], 16)
                sp.dma_start(xt_in[:, b, :], xT_v[:, bass.ds(n, 1), :].squeeze(1)).then_inc(xt_loaded[b], 16)

            def store(h, u):
                sp.wait_ge(out_ready, NT * h + u + 1)
                sp.dma_start(out_v[:, bass.ds(GB * h, GB), u, :], outb[:, u % 2, :, :]).then_inc(slot_free[u % 2], 16)

            sp.dma_start(alpha_in[:, :], alpha.rearrange("(p t) -> p t", t=NT)).then_inc(alpha_loaded, 16)
            for t in range(NT):
                sp.dma_start(adj_in[:, t, :], adj.rearrange("(p t) m -> p t m", t=NT)[:, t, :]).then_inc(adj_loaded[t], 16)
            sp.dma_start(fcw_in[:, :], fcw).then_inc(fcw_loaded, 16)
            sp.dma_start(b_in[:, :], bin_.rearrange("(p a) -> p a", a=1)).then_inc(b_loaded, 16)
            for b in range(GB):
                load(0, b)
            sp.dma_start(nv1_in[:, :, :], nv1T.rearrange("r (t p) -> r t p", t=NT)).then_inc(nv_loaded, 16)
            sp.dma_start(nv2_in[:, :], nv2).then_inc(nv_loaded, 16)
            w_rows = W.rearrange("(m d) e -> d m e", d=D)
            sp.dma_start(wp[:, 0:3, :], w_rows[:, 0:3, :]).then_inc(wp_loaded, 16)
            sp.dma_start(wp_more[:, :, :], w_rows[:, 3:5, :]).then_inc(wp_loaded, 16)
            sp.dma_start(wp[:, 3:5, :], w_rows[:, 5:7, :]).then_inc(wp_loaded, 16)
            sp.dma_start(bias_out[:, :, :], bout.rearrange("p (t e) -> p t e", t=2)).then_inc(bout_loaded, 16)
            for b in range(GB):
                load(1, b)
            with sp.Fori(2, G) as g:
                for b in range(GB):
                    load(g, b)
                    store(g - 2, b)
            for h in (G - 2, G - 1):
                for u in range(NT):
                    store(h, u)
            for i in range(2):
                sp.wait_ge(slot_free[i], 16 * (1 + G * NT // 2))

        @block.scalar
        def _(act):
            for dst, src, loaded in (
                    (wT_in[:, :], wT, w_loaded),
                    (dcol[:, 0:1], dvec.rearrange("(p a) -> p a", a=1), d_loaded)):
                act.dma_start(dst, src).then_inc(loaded, 16)
            act.wait_ge(alpha_loaded, 16)
            nc.scalar.activation(esum[:, :, 0], alpha_in[:, :], ACT.Exp, scale=-1.0).then_inc(gate_exp, 1)

            def power_of_c(n, lo, hi, src):
                act.wait_ge(cp_made, n)
                nc.scalar.activation(CP[:, lo:hi, :].rearrange("p k d -> p (k d)"), src,
                                     ACT.Copy).then_inc(cp_copied, 1)

            power_of_c(1, 1, 2, turn[:, 0:D])
            power_of_c(2, 2, 3, turn[:, D:2 * D])

            def a_split(g):
                for t in range(NT):
                    nc.scalar.activation(As[0][:, t, :], A[:, t, :], ACT.Copy).then_inc(a_high, 1)

            def power_high(k, mt, bank):
                nc.scalar.activation(TA[k - 1][0][:, mt, :], bank, ACT.Copy).then_inc(t_high, 1)

            def a_turned(g):
                for mt in range(NT):
                    act.wait_ge(at_turned, mt + 1)
                    power_high(1, mt, (left + right)[mt][:, :])

            def power2(g, mt):
                act.wait_ge(t_made, mt + 1)
                power_high(2, mt, A2_BANKS[mt])

            def r_high(g):
                act.wait_ge(r_level, STEPS + 1)
                nc.scalar.activation(RC[0][:, :, :], RF[:, :, :, :].rearrange("p i j d -> p i (j d)"),
                                     ACT.Copy).then_inc(rc_high, 1)

            def power3(g, mt):
                act.wait_ge(t_made, NT + mt + 1)
                power_high(3, mt, wide[:, mt % 2, :])

            def soft(g, t):
                act.wait_ge(zneg_done, t + 1)
                nc.scalar.activation(prob[:, 0, :], relu[:, :], ACT.Exp, bias=zneg[:, t:t + 1],
                                     accum_out=zsum[:, t:t + 1]).then_inc(z_exp, 1)
                act.wait_ge(zrec_done, t + 1)
                nc.scalar.activation(prob[:, 1, :], prob[:, 0, :], ACT.Copy, scale=zrec[:, t:t + 1],
                                     accum_out=a1[:, t:t + 1]).then_inc(a_done, 1)

            def wp_high(g):
                act.wait_ge(wp_step, 2)
                nc.scalar.activation(WC[0][:, :], wp[:, :, :].rearrange("p m d -> p (m d)"),
                                     ACT.Copy).then_inc(wc_high, 1)

            def split_x(g, b):
                n = GB * g + b
                act.wait_ge(x_loaded[b], 16 * g + 16)
                if not (isinstance(n, int) and n < 2):
                    act.wait_ge(y_made, y_use(2, b - 2, g) + 1 if b >= 2 else 2 * n - 2)
                nc.scalar.activation(xs[0][:, b % 2, :, :].rearrange("p t d -> p (t d)"), x_in[:, b, :],
                                     ACT.Copy).then_inc(xs_high, 1)

            def split_xT(g, b):
                n = GB * g + b
                act.wait_ge(xt_loaded[b], 16 * g + 16)
                if not (isinstance(n, int) and n < 2):
                    act.wait_ge(right_made, NT * (n - 1))
                nc.scalar.activation(yT[0][0][:, b % 2, :], xt_in[:, b, :], ACT.Copy).then_inc(xts_high, 1)

            def y_high(i):
                def stage(g, b):
                    act.wait_ge(y_made, y_use(i, b, g) + 1)
                    nc.scalar.activation(yT[i][0][:, b % 2, :], left_bank((f"y{i}", b), g)[:, :],
                                         ACT.Copy).then_inc(yT_high, 1)
                return stage

            def inner(g, b, t):
                at = NT * (GB * g + b) + t
                act.wait_ge(right_made, at + 1)
                bank = right[t % 2]
                nc.scalar.activation(Z2[0][:, t, b * D:(b + 1) * D], bank[:, 2 * D:3 * D],
                                     ACT.Copy)
                nc.scalar.activation(Z1[:, t, b, :], bank[:, D:2 * D], ACT.Copy).then_inc(inner_mid, 1)

            def outer1(g, t):
                act.wait_ge(left_drained, left_use(("O1", t), g) + 1)
                nc.scalar.activation(U[0][:, t, :], Z1[:, t, :, :].rearrange("p b d -> p (b d)"),
                                     ACT.Copy).then_inc(u_high, 1)

            def root(ln, stat, made):
                def stage(g, u):
                    act.wait_ge(stat, STAT * (NT * (g - 1) + u + 1))
                    nc.scalar.activation(ln["sd"][:, u % 2, :], ln["mv"][:, u % 2, :, 1], ACT.Sqrt,
                                         bias=eps_c[:, :]).then_inc(made, 1)
                return stage

            def scale(ln, b, u, dst, src):
                return nc.scalar.activation(dst, src, ACT.Identity, bias=ln["nb"][:, u % 2, b:b + 1],
                                            scale=ln["r"][:, u % 2, b:b + 1])

            def scale1(g, u):
                act.wait_ge(ln1_norm, NORM * (NT * (g - 1) + u + 1))
                for b in range(GB):
                    last = scale(LN[0], b, u, x2[:, u, b, :], x2[:, u, b, :])
                last.then_inc(x2_ready, 1)

            def turned(g, u):
                q = NT * (g - 1) + u
                act.wait_ge(turn_made, q + 1)
                nc.scalar.activation(x2T[0][:, u % 2, :, :].rearrange("p b d -> p (b d)"), turn[:, :],
                                     ACT.Copy).then_inc(x2T_high, 1)

            def mix(g, u, half):
                at = 2 * (NT * (g - 1) + u) + half
                act.wait_ge(wide_made, at + 1)
                if u or half:
                    act.wait_ge(res_full, at)
                for m, factor in enumerate((a1, a2)):
                    last = nc.scalar.activation(adapt[:, m, :, :], tail_v[:, :, m * D:(m + 1) * D],
                                                ACT.Copy, scale=factor[:, u:u + 1])
                last.then_inc(tail_taken, 1)

            def scale2(g, u):
                act.wait_ge(ln2_norm, NORM * (NT * (g - 1) + u + 1))
                act.wait_ge(slot_free[u % 2], 16 * (NT // 2 * (g - 1) + u // 2 + 1))
                for b in range(GB):
                    last = scale(LN[1], b, u, outb[:, u % 2, b, :], res[:, u % 2, b, :])
                last.then_inc(out_ready, 1)

            run(act, {"AT": a_turned, "A": a_split, "A2": power2, "RC": r_high,
                      "C34": lambda g: power_of_c(3, 3, 5, turn[:, 2 * D:4 * D]),
                      "C58": lambda g: power_of_c(4, 5, 9, tail[:, :]),
                      "A3": power3, "soft": soft, "wp": wp_high, "splitx": split_x, "splitxT": split_xT,
                      "y1": y_high(1), "y2": y_high(2), "R": inner, "O1": outer1,
                      "stat1": root(LN[0], ln1_stat, ln1_root), "scale1": scale1, "T": turned, "W": mix,
                      "stat2": root(LN[1], ln2_stat, ln2_root), "scale2": scale2})

        @block.gpsimd
        def _(pool):
            nc.gpsimd.memset(ident[:, :], 0.0).then_inc(ident_step, 1)
            nc.gpsimd.memset(eps_c[:, :], EPS).then_inc(ident_step, 1)
            pool.wait_ge(ident_step, 2)
            nc.gpsimd.affine_select(out=ident[:, :], in_=ident[:, :], compare_op=ALU.not_equal, fill=1.0,
                                    base=0, pattern=[[-1, P]], channel_multiplier=1).then_inc(ident_step, 1)
            for i in range(2):
                nc.gpsimd.memset(outb[:, i, :, :], 0.0).then_inc(slot_free[i], 16)
            def wp_low(g):
                pool.wait_ge(ident_step, 3)
                pool.wait_ge(wp_loaded, 48)
                nc.gpsimd.tensor_tensor(wp[:, 0, :], wp[:, 0, :], ident[:, :], ALU.add).then_inc(wp_step, 1)
                nc.gpsimd.tensor_tensor(wp[:, 1:3, :], wp[:, 1:3, :], wp_more[:, :, :], ALU.add).then_inc(wp_step, 1)
                pool.wait_ge(wc_high, 1)
                nc.gpsimd.tensor_tensor(WC[1][:, :], wp[:, :, :].rearrange("p m d -> p (m d)"),
                                        f32(WC[0][:, :]), ALU.subtract).then_inc(wc_low, 1)

            def split_x(g, b):
                n = GB * g + b
                pool.wait_ge(xs_high, n + 1)
                nc.gpsimd.tensor_tensor(xs[1][:, b % 2, :, :].rearrange("p t d -> p (t d)"), x_in[:, b, :],
                                        f32(xs[0][:, b % 2, :, :].rearrange("p t d -> p (t d)")),
                                        ALU.subtract).then_inc(xs_low, 1)

            def split_xT(g, b):
                n = GB * g + b
                pool.wait_ge(xts_high, n + 1)
                nc.gpsimd.tensor_tensor(yT[0][1][:, b % 2, :], xt_in[:, b, :], f32(yT[0][0][:, b % 2, :]),
                                        ALU.subtract).then_inc(xts_low, 1)

            def outer1(g, t):
                pool.wait_ge(u_high, NT * (g - 1) + t + 1)
                nc.gpsimd.tensor_tensor(U[1][:, t, :], Z1[:, t, :, :].rearrange("p b d -> p (b d)"),
                                        f32(U[0][:, t, :]), ALU.subtract).then_inc(u_low, 1)

            def base(g, t):
                if isinstance(g, int):
                    pool.wait_ge(gb_copied, 1)
                pool.wait_ge(inner_base, NT * (GB * g + GB - 1) + t + 1)
                nc.gpsimd.tensor_tensor(
                    Z0[:, t, :, :], Z0[:, t, :, :],
                    g_bias[:, t, :].unsqueeze(1).to_broadcast([P, GB, D]), ALU.add).then_inc(base_full, 1)

            def mix(g, u, half):
                at = 2 * (NT * (g - 1) + u) + half
                r = res[:, u % 2, 2 * half:2 * half + 2, :]
                pool.wait_ge(tail_taken, at + 1)
                nc.gpsimd.tensor_tensor(adapt[:, 0, :, :], adapt[:, 0, :, :], adapt[:, 1, :, :],
                                        ALU.add).then_inc(adapt_sum, 1)
                pool.wait_ge(adapt_sum, at + 1)
                pool.wait_ge(mixed, MIX * (at + 1))
                nc.gpsimd.tensor_tensor(r, r, adapt[:, 0, :, :], ALU.add).then_inc(res_full, 1)

            run(pool, {"W": mix, "wp": wp_low, "splitx": split_x, "splitxT": split_xT, "O1": outer1, "base": base})

        @block.vector
        def _(dve):
            v = nc.vector
            dve.wait_ge(ident_step, 3)
            v.tensor_scalar(CP[:, 0, :], ident[:, :], 1.0, None, ALU.mult).then_inc(cp_copied, 1)
            v.tensor_scalar(identdt[:, :], ident[:, :], DT, None, ALU.mult).then_inc(r_level, 1)
            dve.wait_ge(d_loaded, 16)
            v.tensor_scalar(dcol[:, 1:2], dcol[:, 0:1], 0.0, 1.0, ALU.max, ALU.min).then_inc(d_step, 1)
            dve.wait_ge(d_step, 1)
            dve.wait_ge(w_loaded, 16)
            v.tensor_scalar(wTs[:, :], wT_in[:, :], dcol[:, 1:2], DT, ALU.mult, ALU.mult).then_inc(d_step, 1)
            dve.wait_ge(gate_exp, 1)
            v.tensor_scalar(esum[:, :, 1], esum[:, :, 0], 1.0, None, ALU.add).then_inc(gate_step, 1)
            dve.wait_ge(gate_step, 1)
            v.reciprocal(esum[:, :, 2], esum[:, :, 1]).then_inc(gate_step, 1)
            dve.wait_ge(gate_step, 2)
            v.tensor_scalar(gcol[:, :], esum[:, :, 2], 0.5 * DT, None, ALU.mult).then_inc(gate_step, 1)
            v.tensor_scalar(ccol[:, :], esum[:, :, 2], -0.5 * DT, 1.0 - DT, ALU.mult, ALU.add).then_inc(gate_step, 1)
            dve.wait_ge(gate_step, 4)
            for t in range(NT):
                dve.wait_ge(adj_loaded[t], 16)
                last = v.tensor_scalar(A[:, t, :].rearrange("p (b a) -> p b a", b=NT),
                                       adj_in[:, t, :].rearrange("p (a b) -> p b a", b=NT),
                                       gcol[:, t:t + 1], None, ALU.mult)
            last.then_inc(a_step, 1)
            dve.wait_ge(a_step, 1)
            for t in range(NT):
                last = v.scalar_tensor_tensor(A[:, t, t * P:(t + 1) * P], ident[:, :], ccol[:, t:t + 1],
                                              A[:, t, t * P:(t + 1) * P], ALU.mult, ALU.add)
            last.then_inc(a_step, 1)

            def a_turned(g):
                for mt in range(NT):
                    dve.wait_ge(t_high, mt + 1)
                    v.tensor_tensor(TA[0][1][:, mt, :], (left + right)[mt][:, :], f32(TA[0][0][:, mt, :]),
                                    ALU.subtract).then_inc(t_low, 1)

            def a_split(g):
                for t in range(NT):
                    dve.wait_ge(a_high, t + 1)
                    v.tensor_tensor(As[1][:, t, :], A[:, t, :], f32(As[0][:, t, :]),
                                    ALU.subtract).then_inc(a_low, 1)

            def power2(g, mt):
                dve.wait_ge(t_high, NT + mt + 1)
                v.tensor_tensor(TA[1][1][:, mt, :], A2_BANKS[mt], f32(TA[1][0][:, mt, :]),
                                ALU.subtract).then_inc(t_low, 1)

            def r_sum(g):
                dve.wait_ge(cp_copied, 5)
                for p in range(1, STEPS):
                    dve.wait_ge(r_level, p)
                    for k in range(STEPS - p):
                        acc = RF[:, k % I3, k // I3, :]
                        last = v.scalar_tensor_tensor(acc, CP[:, p, :], DT * comb(k + p, k),
                                                      identdt[:, :] if p == 1 else acc, ALU.mult, ALU.add)
                    last.then_inc(r_level, 1)

            def r_all(g):
                dve.wait_ge(r_level, STEPS)
                dve.wait_ge(fc_made, 3)
                dve.wait_ge(q_made, 1)
                for k in range(STEPS + 1):
                    p = STEPS - k
                    acc = RF[:, k % I3, k // I3, :]
                    fc = wide[:, p // 4, (p % 4) * D:(p % 4 + 1) * D] if p < STEPS else turn[:, 0:D]
                    if k == STEPS:
                        last = v.tensor_copy(acc, fc)
                    else:
                        last = v.scalar_tensor_tensor(acc, fc, float(comb(STEPS, k)),
                                                      acc if k < STEPS - 1 else identdt[:, :], ALU.mult, ALU.add)
                last.then_inc(r_level, 1)
                dve.wait_ge(rc_high, 1)
                v.tensor_tensor(RC[1][:, :, :], RF[:, :, :, :].rearrange("p i j d -> p i (j d)"),
                                f32(RC[0][:, :, :]), ALU.subtract).then_inc(rc_low, 1)

            def vec_split(r):
                dve.wait_ge(v_step, 3 * r + 1)
                v.tensor_copy(Vs[0][:, r, :, :], V[:, :, NV * r:NV * r + NV]).then_inc(v_step, 1)
                dve.wait_ge(v_step, 3 * r + 2)
                v.tensor_tensor(Vs[1][:, r, :, :], V[:, :, NV * r:NV * r + NV], f32(Vs[0][:, r, :, :]),
                                ALU.subtract).then_inc(v_step, 1)

            def power3(g, mt):
                dve.wait_ge(t_high, 2 * NT + mt + 1)
                v.tensor_tensor(TA[2][1][:, mt, :], wide[:, mt % 2, :], f32(TA[2][0][:, mt, :]),
                                ALU.subtract).then_inc(t_low, 1)
                if mt == 0:
                    v.tensor_reduce(s1[:, :], adj_in, AX.X, ALU.add).then_inc(rowsum_done, 1)
                    v.memset(V[:, :, :], 1.0).then_inc(rowsum_done, 1)
                    v.memset(Qc[:, :], 0.0).then_inc(rowsum_done, 1)
                    dve.wait_ge(rowsum_done, 3)
                    v.tensor_tensor(V[:, :, 1], s1[:, :], gcol[:, :], ALU.mult).then_inc(rowsum_done, 1)
                    v.tensor_tensor(s2[:, :], s1[:, :], s1[:, :], ALU.mult)
                    dve.wait_ge(rowsum_done, 4)
                    v.tensor_tensor(V[:, :, 1], V[:, :, 1], ccol[:, :], ALU.add).then_inc(rowsum_done, 1)
                    dve.wait_ge(rowsum_done, 5)
                    v.tensor_copy(Vs[0][:, 1, :, :], V[:, :, 0:NV]).then_inc(rowsum_done, 1)
                    dve.wait_ge(rowsum_done, 6)
                    v.tensor_tensor(Vs[1][:, 1, :, :], V[:, :, 0:NV], f32(Vs[0][:, 1, :, :]),
                                    ALU.subtract).then_inc(rowsum_done, 1)
                    dve.wait_ge(q_made, 1)
                    for k in range(STEPS + 1):
                        src = turn[:, D + STEPS - k:D + STEPS - k + 1]
                        last = v.tensor_scalar(Qc[:, k + k // I3:k + k // I3 + 1], src,
                                               float(comb(STEPS, k)), None, ALU.mult)
                    last.then_inc(q_scaled, 1)

            def vec(g, r):
                dve.wait_ge(v_made, r + 1)
                v.tensor_copy(Vrow[:, VROW[r], :], wide[0:NV, r % 2, :]).then_inc(v_rows, 1)

            def vec_back(g, r):
                dve.wait_ge(v_back, r + 1)
                made = turn[:, 256 + 64 * r:256 + 64 * r + NT * NV].rearrange("p (t c) -> p t c", t=NT)
                if r == 0:
                    v.tensor_copy(V[:, :, 2], made[:, :, 1]).then_inc(v_step, 1)
                else:
                    v.tensor_copy(V[:, :, NV * r:NV * r + NV], made).then_inc(v_step, 1)
                vec_split(r)

            def vecT(g):
                dve.wait_ge(q_turned, 1)
                v.tensor_copy(Qrow[:, :, :].rearrange("k j d -> k (j d)"),
                              turn[0:NV, 0:I3 * D]).then_inc(q_copied, 1)
                dve.wait_ge(v_turned, 1)
                v.tensor_copy(Vrow[:, 0, :], wide[0:NV, 1, :]).then_inc(v_copied, 1)

            def bias_part(g):
                dve.wait_ge(gb_made, 1)
                v.tensor_copy(g_bias[:, :, :].rearrange("p t d -> p (t d)"), wide[:, 1, :]).then_inc(gb_copied, 1)

            def soft(g, t):
                dve.wait_ge(z_made, t + 1)
                if t >= 1:
                    dve.wait_ge(z_exp, t)
                v.tensor_scalar(relu[:, :], tail[:, :], 0.0, None, ALU.max).then_inc(relu_done, 1)
                dve.wait_ge(relu_done, t + 1)
                v.tensor_reduce(zmax[:, t:t + 1], relu[:, :], AX.X, ALU.max).then_inc(a_step, 1)
                dve.wait_ge(a_step, 2 + t + 1)
                v.tensor_scalar(zneg[:, t:t + 1], zmax[:, t:t + 1], -1.0, None, ALU.mult).then_inc(zneg_done, 1)
                dve.wait_ge(z_exp, t + 1)
                v.reciprocal(zrec[:, t:t + 1], zsum[:, t:t + 1]).then_inc(zrec_done, 1)

            def coef(g):
                dve.wait_ge(bout_loaded, 16)
                dve.wait_ge(a_done, NT)
                v.tensor_tensor(a2[:, :], a1[:, :], a1[:, :], ALU.mult).then_inc(coef_done, 1)

            def y_low(i):
                def stage(g, b):
                    dve.wait_ge(yT_high, y_use(i, b, g) + 1)
                    v.tensor_tensor(yT[i][1][:, b % 2, :], left_bank((f"y{i}", b), g)[:, :],
                                    f32(yT[i][0][:, b % 2, :]), ALU.subtract).then_inc(left_drained, 1)
                return stage

            def inner(g, b, t):
                at = NT * (GB * g + b) + t
                bank = right[t % 2]
                dve.wait_ge(inner_mid, at + 1)
                v.tensor_tensor(Z0[:, t, b, :], bank[:, 0:D], x_in[:, b, t * D:(t + 1) * D],
                                ALU.add).then_inc(inner_base, 1)
                v.tensor_tensor(Z2[1][:, t, b * D:(b + 1) * D], bank[:, 2 * D:3 * D],
                                f32(Z2[0][:, t, b * D:(b + 1) * D]), ALU.subtract).then_inc(inner_low, 1)

            def outer1(g, t):
                dve.wait_ge(o1_made, NT * (g - 1) + t + 1)
                dve.wait_ge(inner_mid, NT * GB * g)
                z1 = Z1[:, t, :, :].rearrange("p b d -> p (b d)")
                v.tensor_tensor(z1, left_bank(("O1", t), g)[:, :], z1, ALU.add).then_inc(left_drained, 1)

            def stats(ln, src, u, step, at):
                for b in range(GB):
                    last = v.bn_stats(ln["st"][:, u % 2, b, :], src[:, b, :])
                last.then_inc(step, 1)
                dve.wait_ge(step, at + 1)
                dve.sem_inc(stats_seen)
                for b in range(GB):
                    last = v.bn_aggr(ln["mv"][:, u % 2, b, :], ln["st"][:, u % 2, b, :])
                last.then_inc(step, 1)

            def rsqrt(ln, u, step, at):
                s = u % 2
                r0, q, mv = ln["r0"][:, s, :], ln["q"][:, s, :], ln["mv"][:, s, :, :]
                v.reciprocal(r0, ln["sd"][:, s, :]).then_inc(step, 1)
                dve.wait_ge(step, at + 1)
                v.scalar_tensor_tensor(q, mv[:, :, 1], EPS, r0, ALU.add, ALU.mult).then_inc(step, 1)
                dve.wait_ge(step, at + 2)
                v.scalar_tensor_tensor(ln["q2"][:, s, :], q, -0.5, r0, ALU.mult, ALU.mult).then_inc(step, 1)
                dve.wait_ge(step, at + 3)
                v.scalar_tensor_tensor(ln["r"][:, s, :], ln["q2"][:, s, :], 1.5, r0,
                                       ALU.add, ALU.mult).then_inc(step, 1)
                dve.wait_ge(step, at + 4)
                v.scalar_tensor_tensor(ln["nb"][:, s, :], mv[:, :, 0], -1.0, ln["r"][:, s, :],
                                       ALU.mult, ALU.mult).then_inc(step, 1)

            def outer2(g, u):
                q = NT * (g - 1) + u
                dve.wait_ge(o2_made, q + 1)
                dve.wait_ge(base_full, q + 1)
                v.tensor_tensor(x2[:, u, :, :].rearrange("p b d -> p (b d)"), left_bank(("O2", u), g)[:, :],
                                Z0[:, u, :, :].rearrange("p b d -> p (b d)"), ALU.add).then_inc(left_drained, 1)

            def stat1(g, u):
                dve.wait_ge(left_drained, left_use(("O2", u), g) + 1)
                stats(LN[0], x2[:, u, :, :], u, ln1_stat, STAT * (NT * (g - 1) + u))

            def norm1(g, u):
                q = NT * (g - 1) + u
                dve.wait_ge(ln1_root, q + 1)
                rsqrt(LN[0], u, ln1_norm, NORM * q)

            def turned(g, u):
                dve.wait_ge(x2T_high, NT * (g - 1) + u + 1)
                v.tensor_tensor(x2T[1][:, u % 2, :, :].rearrange("p b d -> p (b d)"), turn[:, :],
                                f32(x2T[0][:, u % 2, :, :].rearrange("p b d -> p (b d)")),
                                ALU.subtract).then_inc(x2T_low, 1)

            def mix(g, u, half):
                at = 2 * (NT * (g - 1) + u) + half
                r = res[:, u % 2, 2 * half:2 * half + 2, :]
                if u >= 2 and half == 0:
                    dve.wait_ge(out_ready, NT * (g - 1) + u - 1)
                dve.wait_ge(wide_made, at + 1)
                v.tensor_tensor(r, wide[:, :, 0:D], bias_out[:, :, :], ALU.add).then_inc(mixed, 1)
                for n, factor in ((1, s1), (2, s2)):
                    dve.wait_ge(mixed, MIX * at + n)
                    v.scalar_tensor_tensor(r, wide[:, :, n * D:(n + 1) * D], factor[:, u:u + 1], r,
                                           ALU.mult, ALU.add).then_inc(mixed, 1)

            def stat2(g, u):
                q = NT * (g - 1) + u
                dve.wait_ge(res_full, 2 * (q + 1))
                stats(LN[1], res[:, u % 2, :, :], u, ln2_stat, STAT * q)

            def norm2(g, u):
                q = NT * (g - 1) + u
                dve.wait_ge(ln2_root, q + 1)
                rsqrt(LN[1], u, ln2_norm, NORM * q)
            run(dve, {"AT": a_turned, "A": a_split, "A2": power2, "Rsum": r_sum, "RC": r_all,
                      "A3": power3, "vec": vec, "vback": vec_back, "vecT": vecT, "gbias": bias_part, "soft": soft,
                      "coef": coef, "y1": y_low(1), "y2": y_low(2), "R": inner, "O1": outer1,
                      "O2": outer2, "stat1": stat1, "norm1": norm1, "T": turned, "W": mix,
                      "stat2": stat2, "norm2": norm2})

        @block.tensor
        def _(pe):
            pe.wait_ge(d_step, 2)
            pe.matmul(turn[:, 0:D], wTs[:, :], wT_in[:, :], start=True, stop=True).then_inc(cp_made, 1)
            pe.wait_ge(cp_copied, 2)
            pe.matmul(turn[:, D:2 * D], CP[:, 1, :], CP[:, 1, :], start=True, stop=True).then_inc(cp_made, 1)

            def c34(g):
                pe.wait_ge(cp_copied, 3)
                pe.matmul(turn[:, 2 * D:4 * D], CP[:, 2, :], CP[:, 1:3, :].rearrange("p k d -> p (k d)"),
                          start=True, stop=True).then_inc(cp_made, 1)

            def c58(g):
                pe.wait_ge(cp_copied, 4)
                pe.matmul(tail[:, :], CP[:, 4, :], CP[:, 1:5, :].rearrange("p k d -> p (k d)"),
                          start=True, stop=True).then_inc(cp_made, 1)

            def a_turned(g):
                pe.wait_ge(a_step, 2)
                for mt in range(NT):
                    for t in range(NT):
                        last = pe.transpose((left + right)[mt][:, t * P:(t + 1) * P],
                                            A[:, t, mt * P:(mt + 1) * P], ident[:, :])
                    last.then_inc(at_turned, 1)

            def fc(g):
                pe.wait_ge(cp_copied, 5)
                pe.wait_ge(fcw_loaded, 16)
                pe.wait_ge(t_low, 2 * NT)
                for lo, hi, bank in ((0, 4, wide[:, 0, :]), (4, 8, wide[:, 1, :]), (8, 9, turn[:, 0:D])):
                    pe.matmul(bank, fcw_in[:, :], CP[:, lo:hi, :].rearrange("p k d -> p (k d)"),
                              start=True, stop=True).then_inc(fc_made, 1)
                pe.wait_ge(b_loaded, 16)
                for p in range(STEPS + 1):
                    last = pe.matmul(turn[:, D + p:D + p + 1], CP[:, p, :], b_in[:, :], start=True, stop=True)
                last.then_inc(q_made, 1)

            def power(k, mt, bank):
                for kt in range(NT):
                    if k == 2 and mt == 0:
                        pe.wait_ge(a_low, kt + 1)
                    last = three(pe, bank, [a[:, kt, mt * P:(mt + 1) * P] for a in As],
                                 [a[:, kt, :] for a in TA[k - 2]], kt == 0, kt == NT - 1)
                last.then_inc(t_made, 1)

            def power2(g, mt):
                power(2, mt, A2_BANKS[mt])

            def power3(g, mt):
                if mt == 0:
                    pe.wait_ge(t_low, 2 * NT)
                    pe.wait_ge(rc_high, 1)
                if mt >= 2:
                    pe.wait_ge(t_low, 2 * NT + mt - 1)
                power(3, mt, wide[:, mt % 2, :])

            def vec(g, r):
                if r == 0:
                    pe.wait_ge(rowsum_done, 7)
                    pe.wait_ge(q_scaled, 1)
                    pe.wait_ge(t_low, 2 * NT + 3)
                else:
                    pe.wait_ge(v_step, 3 * r)
                if r == 1:
                    pe.wait_ge(t_low, 3 * NT)
                src, mats = (1, TA[0]) if r == 0 else (r - 1, TA[2])
                for kt in range(NT):
                    last = three(pe, wide[0:NV, r % 2, :], [a[:, src, kt, :] for a in Vs],
                                 [a[:, kt, :] for a in mats], kt == 0, kt == NT - 1)
                last.then_inc(v_made, 1)

            def vec_back(g, r):
                pe.wait_ge(v_rows, r + 1)
                for t in range(NT):
                    o = 256 + 64 * r + NV * t
                    last = pe.transpose(turn[:, o:o + NV], Vrow[:, VROW[r], t * P:(t + 1) * P],
                                        ident[0:NV, 0:NV])
                last.then_inc(v_back, 1)

            def vecT(g):
                pe.wait_ge(v_step, 6)
                for j in range(I3):
                    last = pe.transpose(turn[0:NV, j * D:(j + 1) * D], Qc[:, j * NV:(j + 1) * NV], ident[:, :])
                last.then_inc(q_turned, 1)
                for t in range(NT):
                    last = pe.transpose(wide[0:NV, 1, t * P:(t + 1) * P], V[:, t, 0:NV], ident[:, :])
                last.then_inc(v_turned, 1)

            def bias_part(g):
                pe.wait_ge(q_copied, 1)
                pe.wait_ge(v_copied, 1)
                pe.wait_ge(v_rows, 3)
                for t in range(NT):
                    for j in range(I3):
                        last = pe.matmul(wide[:, 1, t * D:(t + 1) * D], Vrow[:, j, t * P:(t + 1) * P],
                                         Qrow[:, j, :], start=j == 0, stop=j == I3 - 1)
                last.then_inc(gb_made, 1)

            def soft(g, t):
                if t == 0:
                    pe.wait_ge(nv_loaded, 32)
                else:
                    pe.wait_ge(relu_done, t)
                pe.matmul(tail[:, :], nv1_in[:, t, :], nv2_in[:, :], start=True, stop=True).then_inc(z_made, 1)

            def left_free(stage, g):
                use = left_use(stage, g)
                if isinstance(use, int) and use < 2:
                    return
                pe.wait_ge(left_drained, use - 1)

            def y(i):
                def stage(g, b):
                    pe.wait_ge(xs_low, GB * g + b + 1)
                    if isinstance(g, int) and b == 0:
                        pe.wait_ge(t_low, NT * i)
                    left_free((f"y{i}", b), g)
                    for kt in range(NT):
                        last = three(pe, left_bank((f"y{i}", b), g)[:, :], [a[:, b % 2, kt, :] for a in xs],
                                     [a[:, kt, :] for a in TA[i - 1]], kt == 0, kt == NT - 1)
                    last.then_inc(y_made, 1)
                return stage

            def inner(g, b, t):
                at = NT * (GB * g + b) + t
                if t == 0:
                    pe.wait_ge(xts_low, GB * g + b + 1)
                    pe.wait_ge(left_drained, left_use(("y2", b), g) + 1)
                if isinstance(g, int) and b == 0 and t == 0:
                    pe.wait_ge(rc_low, 1)
                if not (isinstance(at, int) and at < 2):
                    pe.wait_ge(inner_low, at - 1)
                for i in range(I3):
                    last = three(pe, right[t % 2][:, 0:J3 * D], [a[:, b % 2, t * P:(t + 1) * P] for a in yT[i]],
                                 [a[:, i, :] for a in RC], i == 0, i == I3 - 1)
                last.then_inc(right_made, 1)

            def outer(moving, made, name):
                def stage(g, t):
                    left_free((name, t), g)
                    for kt in range(NT):
                        if t == 0 and name == "O1":
                            pe.wait_ge(inner_low, NT * (GB * g - 1) + kt + 1)
                        if t == 0 and name == "O2":
                            pe.wait_ge(u_low, NT * (g - 1) + kt + 1)
                        last = three(pe, left_bank((name, t), g)[:, :],
                                     [a[:, kt, t * P:(t + 1) * P] for a in TA[2]],
                                     [a[:, kt, :] for a in moving], kt == 0, kt == NT - 1)
                    last.then_inc(made, 1)
                return stage

            def turned(g, u):
                q = NT * (g - 1) + u
                pe.wait_ge(x2_ready, q + 1)
                if u:
                    pe.wait_ge(x2T_low, q)
                for b in range(GB):
                    last = pe.transpose(turn[:, b * P:(b + 1) * P], x2[:, u, b, :], ident[:, :])
                last.then_inc(turn_made, 1)

            def mix(g, u, half):
                q = NT * (g - 1) + u
                pe.wait_ge(x2T_low, q + 1)
                if u or half:
                    pe.wait_ge(mixed, MIX * (2 * q + half))
                    pe.wait_ge(tail_taken, 2 * q + half)
                if u == 0 and half == 0:
                    pe.wait_ge(wc_low, 1)
                for t in range(2):
                    weights = [a[:, u % 2, 2 * half + t, :] for a in x2T]
                    three(pe, wide[:, t, 0:PW], weights, [a[:, 0:PW] for a in WC], True, True)
                    last = three(pe, tail_v[:, t, :], weights, [a[:, PW:NP5 * D] for a in WC], True, True)
                last.then_inc(wide_made, 1)

            run(pe, {"C34": c34, "C58": c58, "AT": a_turned, "FC": fc, "A2": power2,
                     "A3": power3, "vec": vec, "vback": vec_back, "vecT": vecT, "gbias": bias_part, "soft": soft,
                     "y1": y(1), "y2": y(2), "R": inner, "O1": outer(Z2, o1_made, "O1"),
                     "O2": outer(U, o2_made, "O2"), "T": turned, "W": mix})


def kernel(x, adj, L0_gnn_alpha_train, L0_gnn_w, L0_gnn_d, L0_gnn_fc_in_w, L0_gnn_fc_in_b,
           L1_gnn_node_vec1, L1_gnn_node_vec2, L1_gnn_W, L1_gnn_b):
    import numpy as np
    import concourse.bacc as bacc
    from concourse.bass_utils import run_bass_kernel_spmd

    B, N, D = x.shape
    T = 4
    x, nv1 = np.asarray(x), np.asarray(L1_gnn_node_vec1)
    arrays = {
        "x": x,
        "xT": x.reshape(B, N // T, T, D).transpose(0, 3, 2, 1).reshape(B, D, N),
        "adj": adj,
        "alpha": L0_gnn_alpha_train,
        "wT": np.asarray(L0_gnn_w).T,
        "dvec": L0_gnn_d,
        "fcw": L0_gnn_fc_in_w,
        "bin": L0_gnn_fc_in_b,
        "nv1T": nv1.reshape(N // T, T, nv1.shape[1]).transpose(2, 1, 0).reshape(nv1.shape[1], N),
        "nv2": L1_gnn_node_vec2,
        "W": L1_gnn_W,
        "bout": np.broadcast_to(np.asarray(L1_gnn_b), (128, 2, D)).reshape(128, 2 * D),
    }
    nc = bacc.Bacc("TRN2", target_bir_lowering=False, num_devices=1)
    feeds, args = {}, []
    for name, a in arrays.items():
        a = np.ascontiguousarray(a)
        feeds[f"in_{name}"] = a
        args.append(nc.dram_tensor(f"in_{name}", a.shape, mybir.dt.from_np(a.dtype), kind="ExternalInput").ap())
    args.append(nc.dram_tensor("out", (B, N, D), mybir.dt.float32, kind="ExternalOutput").ap())
    graph_resnorm_kernel(nc, *args)
    r = run_bass_kernel_spmd(nc, [feeds], core_ids=[0])
    return r.results[0]["out"]
```

```python
import concourse.bass as bass
from concourse import mybir
from contextlib import ExitStack
from math import comb


def graph_resnorm_kernel(nc, x, xT, adj, alpha, wT, dvec, fcw, bin_, nv1T, nv2, W, bout, out):
    F32 = mybir.dt.float32
    F32R = mybir.dt.float32r
    ALU = mybir.AluOpType
    ACT = mybir.ActivationFunctionType
    AX = mybir.AxisListType

    P = nc.NUM_PARTITIONS
    B, N, D = x.shape
    NT = N // P
    GB = 4
    G = B // GB
    RANK = nv1T.shape[0]
    STEPS = 8
    DT = 1.0 / STEPS
    EPS = 1e-5
    I3 = J3 = 3
    NP5 = 5
    PW = 3 * D
    NV = 4
    VROW = (3, 1, 2)

    ctx = ExitStack()
    with ctx:
        def sb(name, shape, dt=F32):
            return ctx.enter_context(nc.sbuf_tensor(name, shape, dt))

        def pb(name, shape, dt=F32):
            return ctx.enter_context(nc.psum_tensor(name, shape, dt))

        def sem(name):
            return ctx.enter_context(nc.semaphore(name))

        def f32(ap):
            return ap.bitcast(F32)

        ident = sb("ident", [P, P])
        identdt = sb("identdt", [P, P])
        TA = [[sb(f"A{k}T_{part}", [P, NT, N], F32R) for part in ("hi", "lo")] for k in (1, 2, 3)]
        RC = [sb(f"R_{part}", [P, I3, J3 * D], F32R) for part in ("hi", "lo")]
        WC = [sb(f"WP_{part}", [P, NP5 * D], F32R) for part in ("hi", "lo")]
        wp = sb("wp", [P, NP5, D])
        wp_more = sb("wp_more", [P, 2, D])
        bias_out = sb("bias_out", [P, 2, D])
        g_bias = sb("g_bias", [P, NT, D])
        s1 = sb("s1", [P, NT])
        s2 = sb("s2", [P, NT])
        a1 = sb("a1", [P, NT])
        a2 = sb("a2", [P, NT])
        eps_c = sb("eps_c", [P, 1])
        root_one = sb("root_one", [P, 1])
        x_in = sb("x_in", [P, GB, NT * D])
        xt_in = sb("xt_in", [P, GB, N])
        xs = [sb(f"x_{part}", [P, 2, NT, D], F32R) for part in ("hi", "lo")]
        yT = [[sb(f"y{i}T_{part}", [P, 2, N], F32R) for part in ("hi", "lo")] for i in range(I3)]
        Z0 = sb("Z0", [P, NT, GB, D])
        Z1 = sb("Z1", [P, NT, GB, D])
        Z2 = [sb(f"Z2_{part}", [P, NT, GB * D], F32R) for part in ("hi", "lo")]
        U = [sb(f"U_{part}", [P, NT, GB * D], F32R) for part in ("hi", "lo")]
        x2 = sb("x2", [P, NT, GB, D])
        x2T = [sb(f"x2T_{part}", [P, 2, GB, D], F32R) for part in ("hi", "lo")]
        res = sb("res", [P, 2, GB, D])
        adapt = sb("adapt", [P, 2, 2, D])
        outb = sb("outb", [P, 2, GB, D])
        LN = [dict({"st": sb(f"st{l}", [P, 2, GB, 6]), "mv": sb(f"mv{l}", [P, 2, GB, 2])},
                   **{name: sb(f"{name}{l}", [P, 2, GB]) for name in ("sd", "r0", "q", "q2", "r", "nb")})
              for l in (1, 2)]
        alpha_in = sb("alpha_in", [P, NT])
        esum = sb("esum", [P, NT, 4])
        gcol = sb("gcol", [P, NT])
        ccol = sb("ccol", [P, NT])
        dcol = sb("dcol", [P, 2])
        wT_in = sb("wT_in", [P, D])
        wTs = sb("wTs", [P, D])
        fcw_in = sb("fcw_in", [P, D])
        b_in = sb("b_in", [P, 1])
        RF = sb("RF", [P, I3, J3, D])
        Qc = sb("Qc", [P, I3, 2, NV])
        Qrow = sb("Qrow", [2 * NV, I3, D])
        fold = sb("fold", [2 * NV, NV])
        V = sb("V", [P, NT, I3 * NV])
        Vs = sb("Vs", [P, I3, NT, 2 * NV], F32R)
        nv1_in = sb("nv1_in", [RANK, NT, P])
        nv2_in = sb("nv2_in", [RANK, N])
        zmax = sb("zmax", [P, NT])
        zneg = sb("zneg", [P, NT])
        zsum = sb("zsum", [P, NT])
        zrec = sb("zrec", [P, NT])
        prob = res[:, :, :, :].rearrange("p s b d -> p s (b d)")
        adj_in = x2[:, :, :, :].rearrange("p t b d -> p t (b d)")
        A = Z0[:, :, :, :].rearrange("p t b d -> p t (b d)")
        As = U
        Vrow = adj_in[0:2 * NV, :, :]
        CP = Z1[:, :, :, :].rearrange("p t b d -> p (t b) d")[:, 0:STEPS + 1, :]
        relu = outb[:, 0, :, :].rearrange("p b d -> p (b d)")

        left = [pb(f"left{i}", [P, 512]) for i in range(2)]
        right_pair = pb("right_pair", [P, 2, 512])
        right = [right_pair[:, i, :] for i in range(2)]
        turn = pb("turn", [P, 512])
        wide = pb("wide", [P, 2, 512])
        tail = pb("tail", [P, 512])
        A2_BANKS = [right[0][:, :], right[1][:, :], wide[:, 0, :], wide[:, 1, :]]
        MIX_BANKS = [(wide, tail[:, :].rearrange("p (t c) -> p t c", t=2)),
                     (right_pair, left[1][:, :].rearrange("p (t c) -> p t c", t=2))]
        ADAPT = [adapt[:, :, :, :], x_in[:, 0, :].rearrange("p (m b d) -> p m b d", m=2, b=2)]

        adj_loaded = [sem(f"adj_loaded{t}") for t in range(NT)]
        w_loaded, d_loaded, fcw_loaded, b_loaded = map(
            sem, ("w_loaded", "d_loaded", "fcw_loaded", "b_loaded"))
        alpha_loaded, nv_loaded, wp_loaded, bout_loaded = map(
            sem, ("alpha_loaded", "nv_loaded", "wp_loaded", "bout_loaded"))
        ident_step, gate_exp, gate_step, d_step, a_step, a_ready = map(
            sem, ("ident_step", "gate_exp", "gate_step", "d_step", "a_step", "a_ready"))
        a_high, a_low, at_turned, t_high, t_low, t_made = map(
            sem, ("a_high", "a_low", "at_turned", "t_high", "t_low", "t_made"))
        cp_made, cp_copied, fc_made, r_level, rc_high, rc_low = map(
            sem, ("cp_made", "cp_copied", "fc_made", "r_level", "rc_high", "rc_low"))
        q_made, q_scaled, q_turned, q_copied = map(sem, ("q_made", "q_scaled", "q_turned", "q_copied"))
        v_step, v_made, v_rows, v_back, v_turned, v_copied, gb_made, gb_copied = map(
            sem, ("v_step", "v_made", "v_rows", "v_back", "v_turned", "v_copied", "gb_made", "gb_copied"))
        wp_step, wc_high, wc_low = map(sem, ("wp_step", "wc_high", "wc_low"))
        z_made, relu_done, zneg_done, z_exp, zrec_done, a_done, coef_done = map(
            sem, ("z_made", "relu_done", "zneg_done", "z_exp", "zrec_done", "a_done", "coef_done"))
        rowsum_done = sem("rowsum_done")
        x_loaded = [sem(f"x_loaded{i}") for i in range(GB)]
        xt_loaded = [sem(f"xt_loaded{i}") for i in range(GB)]
        xs_high, xs_low, xts_high, xts_low = map(sem, ("xs_high", "xs_low", "xts_high", "xts_low"))
        y_made, o1_made, o2_made, left_drained, yT_high = map(
            sem, ("y_made", "o1_made", "o2_made", "left_drained", "yT_high"))
        right_made, inner_mid, inner_base, inner_low = map(
            sem, ("right_made", "inner_mid", "inner_base", "inner_low"))
        u_high, u_low, base_full = map(sem, ("u_high", "u_low", "base_full"))
        ln1_stat, ln1_root, ln1_norm, x2_ready, turn_made, x2T_high, x2T_low = map(
            sem, ("ln1_stat", "ln1_root", "ln1_norm", "x2_ready", "turn_made", "x2T_high", "x2T_low"))
        wide_made, mixed, tail_taken, adapt_sum, res_full, ln2_stat, ln2_root, ln2_norm, out_ready = map(
            sem, ("wide_made", "mixed", "tail_taken", "adapt_sum", "res_full", "ln2_stat", "ln2_root", "ln2_norm", "out_ready"))
        stats_seen = sem("stats_seen")
        slot_free = [sem(f"slot_free{i}") for i in range(2)]
        MIX = 3
        STAT = 2
        NORM = 5

        FIRST = [("splitx", 0), ("AT",), ("C34",), ("A",), ("y1", 0), ("A2", 0), ("Rsum", 1),
                 ("C58",), ("A2", 1), ("Rsum", 2), ("splitx", 1), ("splitxT", 0), ("A2", 2),
                 ("Rsum", 3), ("A2", 3), ("Rsum", 4), ("y1", 1), ("Rsum", 5), ("FC",), ("Rsum", 6),
                 ("Rsum", 7), ("RC",), ("y2", 0), ("splitxT", 1), ("y2", 1), ("splitx", 2),
                 ("R", 0, 0), ("R", 0, 1), ("R", 0, 2), ("R", 0, 3), ("splitxT", 2), ("y1", 2),
                 ("splitx", 3), ("y2", 2), ("A3", 0), ("A3", 1), ("R", 1, 0), ("R", 1, 1),
                 ("A3", 2), ("R", 1, 2), ("A3", 3), ("R", 1, 3), ("splitxT", 3), ("y1", 3),
                 ("soft", 0), ("vec", 0), ("y2", 3), ("vback", 0), ("R", 2, 0), ("vec", 1),
                 ("R", 2, 1), ("soft", 1), ("vback", 1), ("R", 2, 2), ("vec", 2), ("soft", 2),
                 ("R", 2, 3), ("vecT",), ("R", 3, 0), ("soft", 3), ("wp",), ("R", 3, 1),
                 ("gbias",), ("R", 3, 2), ("R", 3, 3), ("coef",), ("base", 0), ("base", 1),
                 ("base", 2), ("base", 3)]
        STEADY = [("sqrt",), ("splitx", 0), ("O1", 0), ("O1", 1), ("O1", 2), ("O1", 3), ("y1", 0),
                  ("y2", 0), ("O2", 0), ("splitxT", 0), ("stat1", 0), ("O2", 1), ("stat1", 1),
                  ("norm1", 0), ("splitx", 1), ("scale1", 0), ("O2", 2), ("stat1", 2), ("R", 0, 0),
                  ("norm1", 1), ("O2", 3), ("R", 0, 1), ("scale1", 1), ("T", 0), ("splitxT", 1),
                  ("stat1", 3), ("R", 0, 2), ("norm1", 2), ("y1", 1), ("splitx", 2), ("W", 0, 0),
                  ("T", 1), ("y2", 1), ("scale1", 2), ("W", 0, 1), ("norm1", 3), ("R", 0, 3),
                  ("y1", 2), ("R", 1, 0), ("W", 1, 0), ("splitx", 3), ("scale1", 3), ("R", 1, 1),
                  ("R", 1, 2), ("stat2", 0), ("W", 1, 1), ("T", 2), ("y2", 2), ("splitxT", 2),
                  ("norm2", 0), ("stat2", 1), ("scale2", 0), ("R", 1, 3), ("W", 2, 0),
                  ("norm2", 1), ("T", 3), ("y1", 3), ("y2", 3), ("splitxT", 3), ("W", 2, 1),
                  ("R", 2, 0), ("R", 2, 1), ("R", 2, 2), ("R", 2, 3), ("scale2", 1), ("stat2", 2),
                  ("R", 3, 0), ("W", 3, 0), ("norm2", 2), ("R", 3, 1), ("R", 3, 2), ("base", 0),
                  ("base", 1), ("W", 3, 1), ("base", 2), ("R", 3, 3), ("stat2", 3), ("norm2", 3),
                  ("scale2", 2), ("base", 3), ("scale2", 3)]
        LAST = [("O1", 0), ("O1", 1), ("O1", 2), ("O1", 3), ("O2", 0), ("stat1", 0), ("norm1", 0),
                ("O2", 1), ("scale1", 0), ("stat1", 1), ("O2", 2), ("norm1", 1), ("T", 0),
                ("scale1", 1), ("stat1", 2), ("O2", 3), ("norm1", 2), ("T", 1), ("W", 0, 0),
                ("scale1", 2), ("stat1", 3), ("W", 0, 1), ("norm1", 3), ("T", 2), ("W", 1, 0),
                ("scale1", 3), ("stat2", 0), ("W", 1, 1), ("norm2", 0), ("T", 3), ("scale2", 0),
                ("stat2", 1), ("W", 2, 0), ("norm2", 1), ("W", 2, 1), ("scale2", 1), ("W", 3, 0),
                ("stat2", 2), ("W", 3, 1), ("norm2", 2), ("scale2", 2), ("stat2", 3), ("norm2", 3),
                ("scale2", 3)]
        LEFT = ("y1", "y2", "O1", "O2")

        def left_uses(order):
            return [s[:2] for s in order if s[0] in LEFT]

        def left_use(stage, g):
            if isinstance(g, int) and g == 0:
                return left_uses(FIRST).index(stage)
            per = len(left_uses(STEADY))
            order = LAST if isinstance(g, int) and g == G else STEADY
            return per * g + (left_uses(FIRST).__len__() - per + left_uses(order).index(stage))

        def is_last(g):
            return isinstance(g, int) and g == G

        def mix_set(g, half):
            return half if is_last(g) else 0

        def mix_before(g, at):
            return at - 1 if is_last(g) else at

        def left_bank(stage, g):
            if is_last(g) and stage == ("O2", NT - 1):
                return left[0]
            order = FIRST if isinstance(g, int) and g == 0 else \
                LAST if isinstance(g, int) and g == G else STEADY
            return left[left_uses(order).index(stage) % 2]

        def y_use(i, b, g):
            order = FIRST if isinstance(g, int) and g == 0 else STEADY
            ys = [s for s in order if s[0] in ("y1", "y2")]
            return len(ys) * g + ys.index((f"y{i}", b))

        def three(pe, bank, weights, moving, first, last):
            pe.matmul(bank, weights[0], moving[0], start=first, stop=False)
            pe.matmul(bank, weights[0], moving[1], start=False, stop=False)
            return pe.matmul(bank, weights[1], moving[0], start=False, stop=last)

        def run(engine, stages):
            for stage in FIRST:
                if stage[0] in stages:
                    stages[stage[0]](0, *stage[1:])
            with engine.Fori(1, G) as g:
                for stage in STEADY:
                    if stage[0] in stages:
                        stages[stage[0]](g, *stage[1:])
            for stage in LAST:
                if stage[0] in stages:
                    stages[stage[0]](G, *stage[1:])

        block = ctx.enter_context(nc.Block())
        x_v = x.rearrange("b (p t) d -> p b (t d)", t=NT)
        xT_v = xT.rearrange("b d n -> d b n")
        out_v = out.rearrange("b (p t) d -> p b t d", t=NT)

        @block.sync
        def _(sp):
            def load(g, b):
                n = GB * g + b
                if not (isinstance(g, int) and g == 0):
                    sp.wait_ge(inner_base, NT * GB * g + NT * (b + 1 - GB))
                sp.dma_start(x_in[:, b, :], x_v[:, bass.ds(n, 1), :].squeeze(1)).then_inc(x_loaded[b], 16)
                sp.dma_start(xt_in[:, b, :], xT_v[:, bass.ds(n, 1), :].squeeze(1)).then_inc(xt_loaded[b], 16)

            def store(h, u):
                sp.wait_ge(out_ready, NT * h + u + 1)
                sp.dma_start(out_v[:, bass.ds(GB * h, GB), u, :], outb[:, u % 2, :, :]).then_inc(slot_free[u % 2], 16)

            sp.dma_start(alpha_in[:, :], alpha.rearrange("(p t) -> p t", t=NT)).then_inc(alpha_loaded, 16)
            for t in range(NT):
                sp.dma_start(adj_in[:, t, :], adj.rearrange("(p t) m -> p t m", t=NT)[:, t, :]).then_inc(adj_loaded[t], 16)
            sp.dma_start(fcw_in[:, :], fcw).then_inc(fcw_loaded, 16)
            sp.dma_start(b_in[:, :], bin_.rearrange("(p a) -> p a", a=1)).then_inc(b_loaded, 16)
            for b in range(GB):
                load(0, b)
            sp.dma_start(nv1_in[:, :, :], nv1T.rearrange("r (t p) -> r t p", t=NT)).then_inc(nv_loaded, 16)
            sp.dma_start(nv2_in[:, :], nv2).then_inc(nv_loaded, 16)
            w_rows = W.rearrange("(m d) e -> d m e", d=D)
            sp.dma_start(wp[:, 0:3, :], w_rows[:, 0:3, :]).then_inc(wp_loaded, 16)
            sp.dma_start(wp_more[:, :, :], w_rows[:, 3:5, :]).then_inc(wp_loaded, 16)
            sp.dma_start(wp[:, 3:5, :], w_rows[:, 5:7, :]).then_inc(wp_loaded, 16)
            sp.dma_start(bias_out[:, :, :], bout.rearrange("p (t e) -> p t e", t=2)).then_inc(bout_loaded, 16)
            for b in range(GB):
                load(1, b)
            with sp.Fori(2, G) as g:
                for b in range(GB):
                    load(g, b)
                    store(g - 2, b)
            for h in (G - 2, G - 1):
                for u in range(NT):
                    store(h, u)
            for i in range(2):
                sp.wait_ge(slot_free[i], 16 * (1 + G * NT // 2))

        @block.scalar
        def _(act):
            for dst, src, loaded in (
                    (wT_in[:, :], wT, w_loaded),
                    (dcol[:, 0:1], dvec.rearrange("(p a) -> p a", a=1), d_loaded)):
                act.dma_start(dst, src).then_inc(loaded, 16)
            act.wait_ge(alpha_loaded, 16)
            nc.scalar.activation(esum[:, :, 0], alpha_in[:, :], ACT.Exp, scale=-1.0).then_inc(gate_exp, 1)

            def power_of_c(n, lo, hi, src):
                act.wait_ge(cp_made, n)
                nc.scalar.activation(CP[:, lo:hi, :].rearrange("p k d -> p (k d)"), src,
                                     ACT.Copy).then_inc(cp_copied, 1)

            power_of_c(1, 1, 2, turn[:, 0:D])
            power_of_c(2, 2, 3, turn[:, D:2 * D])

            def a_split(g):
                for t in range(NT):
                    nc.scalar.activation(As[0][:, t, :], A[:, t, :], ACT.Copy).then_inc(a_high, 1)

            def power_high(k, mt, bank):
                nc.scalar.activation(TA[k - 1][0][:, mt, :], bank, ACT.Copy).then_inc(t_high, 1)

            def a_turned(g):
                for mt in range(NT):
                    act.wait_ge(at_turned, mt + 1)
                    power_high(1, mt, (left + right)[mt][:, :])

            def power2(g, mt):
                act.wait_ge(t_made, mt + 1)
                power_high(2, mt, A2_BANKS[mt])

            def r_high(g):
                act.wait_ge(r_level, STEPS + 1)
                nc.scalar.activation(RC[0][:, :, :], RF[:, :, :, :].rearrange("p i j d -> p i (j d)"),
                                     ACT.Copy).then_inc(rc_high, 1)

            def power3(g, mt):
                act.wait_ge(t_made, NT + mt + 1)
                power_high(3, mt, wide[:, mt % 2, :])

            def soft(g, t):
                act.wait_ge(zneg_done, t + 1)
                nc.scalar.activation(prob[:, 0, :], relu[:, :], ACT.Exp, bias=zneg[:, t:t + 1],
                                     accum_out=zsum[:, t:t + 1]).then_inc(z_exp, 1)
                act.wait_ge(zrec_done, t + 1)
                nc.scalar.activation(prob[:, 1, :], prob[:, 0, :], ACT.Copy, scale=zrec[:, t:t + 1],
                                     accum_out=a1[:, t:t + 1]).then_inc(a_done, 1)

            def wp_high(g):
                act.wait_ge(wp_step, 2)
                nc.scalar.activation(WC[0][:, :], wp[:, :, :].rearrange("p m d -> p (m d)"),
                                     ACT.Copy).then_inc(wc_high, 1)

            def split_x(g, b):
                n = GB * g + b
                act.wait_ge(x_loaded[b], 16 * g + 16)
                if not (isinstance(n, int) and n < 2):
                    act.wait_ge(y_made, y_use(2, b - 2, g) + 1 if b >= 2 else 2 * n - 2)
                nc.scalar.activation(xs[0][:, b % 2, :, :].rearrange("p t d -> p (t d)"), x_in[:, b, :],
                                     ACT.Copy).then_inc(xs_high, 1)

            def split_xT(g, b):
                n = GB * g + b
                act.wait_ge(xt_loaded[b], 16 * g + 16)
                if not (isinstance(n, int) and n < 2):
                    act.wait_ge(right_made, NT * (n - 1))
                nc.scalar.activation(yT[0][0][:, b % 2, :], xt_in[:, b, :], ACT.Copy).then_inc(xts_high, 1)

            def y_high(i):
                def stage(g, b):
                    act.wait_ge(y_made, y_use(i, b, g) + 1)
                    nc.scalar.activation(yT[i][0][:, b % 2, :], left_bank((f"y{i}", b), g)[:, :],
                                         ACT.Copy).then_inc(yT_high, 1)
                return stage

            def inner(g, b, t):
                at = NT * (GB * g + b) + t
                act.wait_ge(right_made, at + 1)
                bank = right[t % 2]
                nc.scalar.activation(Z2[0][:, t, b * D:(b + 1) * D], bank[:, 2 * D:3 * D],
                                     ACT.Copy)
                nc.scalar.activation(Z1[:, t, b, :], bank[:, D:2 * D], ACT.Copy).then_inc(inner_mid, 1)

            def outer1(g, t):
                act.wait_ge(left_drained, left_use(("O1", t), g) + 1)
                nc.scalar.activation(U[0][:, t, :], Z1[:, t, :, :].rearrange("p b d -> p (b d)"),
                                     ACT.Copy).then_inc(u_high, 1)

            def root(ln, stat, made):
                def stage(g, u):
                    act.wait_ge(stat, STAT * (NT * (g - 1) + u + 1))
                    nc.scalar.activation(ln["sd"][:, u % 2, :], ln["mv"][:, u % 2, :, 1], ACT.Sqrt,
                                         bias=eps_c[:, :]).then_inc(made, 1)
                return stage

            def scale(ln, b, u, dst, src):
                return nc.scalar.activation(dst, src, ACT.Identity, bias=ln["nb"][:, u % 2, b:b + 1],
                                            scale=ln["r"][:, u % 2, b:b + 1])

            def scale1(g, u):
                act.wait_ge(ln1_norm, NORM * (NT * (g - 1) + u + 1))
                for b in range(GB):
                    last = scale(LN[0], b, u, x2[:, u, b, :], x2[:, u, b, :])
                last.then_inc(x2_ready, 1)

            def turned(g, u):
                q = NT * (g - 1) + u
                act.wait_ge(turn_made, q + 1)
                nc.scalar.activation(x2T[0][:, u % 2, :, :].rearrange("p b d -> p (b d)"), turn[:, :],
                                     ACT.Copy).then_inc(x2T_high, 1)

            def mix(g, u, half):
                at = 2 * (NT * (g - 1) + u) + half
                act.wait_ge(wide_made, at + 1)
                if u or (half and not is_last(g)):
                    act.wait_ge(res_full, mix_before(g, at))
                tail_v, parts = MIX_BANKS[mix_set(g, half)][1], ADAPT[mix_set(g, half)]
                for m, factor in enumerate((a1, a2)):
                    last = nc.scalar.activation(parts[:, m, :, :], tail_v[:, :, m * D:(m + 1) * D],
                                                ACT.Copy, scale=factor[:, u:u + 1])
                last.then_inc(tail_taken, 1)

            def scale2(g, u):
                act.wait_ge(ln2_norm, NORM * (NT * (g - 1) + u + 1))
                act.wait_ge(slot_free[u % 2], 16 * (NT // 2 * (g - 1) + u // 2 + 1))
                for b in range(GB):
                    last = scale(LN[1], b, u, outb[:, u % 2, b, :], res[:, u % 2, b, :])
                last.then_inc(out_ready, 1)

            def sqrt_table(g):
                nc.scalar.activation(root_one[:, :], eps_c[:, :], ACT.Sqrt)

            run(act, {"sqrt": sqrt_table, "AT": a_turned, "A": a_split, "A2": power2, "RC": r_high,
                      "C34": lambda g: power_of_c(3, 3, 5, turn[:, 2 * D:4 * D]),
                      "C58": lambda g: power_of_c(4, 5, 9, tail[:, :]),
                      "A3": power3, "soft": soft, "wp": wp_high, "splitx": split_x, "splitxT": split_xT,
                      "y1": y_high(1), "y2": y_high(2), "R": inner, "O1": outer1,
                      "stat1": root(LN[0], ln1_stat, ln1_root), "scale1": scale1, "T": turned, "W": mix,
                      "stat2": root(LN[1], ln2_stat, ln2_root), "scale2": scale2})

        @block.gpsimd
        def _(pool):
            nc.gpsimd.memset(ident[:, :], 0.0).then_inc(ident_step, 1)
            nc.gpsimd.memset(eps_c[:, :], EPS).then_inc(ident_step, 1)
            pool.wait_ge(ident_step, 2)
            nc.gpsimd.affine_select(out=ident[:, :], in_=ident[:, :], compare_op=ALU.not_equal, fill=1.0,
                                    base=0, pattern=[[-1, P]], channel_multiplier=1).then_inc(ident_step, 1)
            for i in range(2):
                nc.gpsimd.memset(outb[:, i, :, :], 0.0).then_inc(slot_free[i], 16)
            def wp_low(g):
                pool.wait_ge(ident_step, 3)
                pool.wait_ge(wp_loaded, 48)
                nc.gpsimd.tensor_tensor(wp[:, 0, :], wp[:, 0, :], ident[:, :], ALU.add).then_inc(wp_step, 1)
                nc.gpsimd.tensor_tensor(wp[:, 1:3, :], wp[:, 1:3, :], wp_more[:, :, :], ALU.add).then_inc(wp_step, 1)
                pool.wait_ge(wc_high, 1)
                nc.gpsimd.tensor_tensor(WC[1][:, :], wp[:, :, :].rearrange("p m d -> p (m d)"),
                                        f32(WC[0][:, :]), ALU.subtract).then_inc(wc_low, 1)

            def split_x(g, b):
                n = GB * g + b
                pool.wait_ge(xs_high, n + 1)
                nc.gpsimd.tensor_tensor(xs[1][:, b % 2, :, :].rearrange("p t d -> p (t d)"), x_in[:, b, :],
                                        f32(xs[0][:, b % 2, :, :].rearrange("p t d -> p (t d)")),
                                        ALU.subtract).then_inc(xs_low, 1)

            def split_xT(g, b):
                n = GB * g + b
                pool.wait_ge(xts_high, n + 1)
                nc.gpsimd.tensor_tensor(yT[0][1][:, b % 2, :], xt_in[:, b, :], f32(yT[0][0][:, b % 2, :]),
                                        ALU.subtract).then_inc(xts_low, 1)

            def outer1(g, t):
                pool.wait_ge(u_high, NT * (g - 1) + t + 1)
                nc.gpsimd.tensor_tensor(U[1][:, t, :], Z1[:, t, :, :].rearrange("p b d -> p (b d)"),
                                        f32(U[0][:, t, :]), ALU.subtract).then_inc(u_low, 1)

            def base(g, t):
                if isinstance(g, int):
                    pool.wait_ge(gb_copied, 1)
                pool.wait_ge(inner_base, NT * (GB * g + GB - 1) + t + 1)
                nc.gpsimd.tensor_tensor(
                    Z0[:, t, :, :], Z0[:, t, :, :],
                    g_bias[:, t, :].unsqueeze(1).to_broadcast([P, GB, D]), ALU.add).then_inc(base_full, 1)

            def mix(g, u, half):
                at = 2 * (NT * (g - 1) + u) + half
                r = res[:, u % 2, 2 * half:2 * half + 2, :]
                pool.wait_ge(tail_taken, at + 1)
                parts = ADAPT[mix_set(g, half)]
                nc.gpsimd.tensor_tensor(parts[:, 0, :, :], parts[:, 0, :, :], parts[:, 1, :, :],
                                        ALU.add).then_inc(adapt_sum, 1)
                pool.wait_ge(adapt_sum, at + 1)
                pool.wait_ge(mixed, MIX * (at + 1))
                nc.gpsimd.tensor_tensor(r, r, parts[:, 0, :, :], ALU.add).then_inc(res_full, 1)

            run(pool, {"W": mix, "wp": wp_low, "splitx": split_x, "splitxT": split_xT, "O1": outer1, "base": base})

        @block.vector
        def _(dve):
            v = nc.vector
            dve.wait_ge(ident_step, 3)
            v.tensor_scalar(CP[:, 0, :], ident[:, :], 1.0, None, ALU.mult).then_inc(cp_copied, 1)
            v.tensor_scalar(identdt[:, :], ident[:, :], DT, None, ALU.mult).then_inc(r_level, 1)
            dve.wait_ge(d_loaded, 16)
            v.tensor_scalar(dcol[:, 1:2], dcol[:, 0:1], 0.0, 1.0, ALU.max, ALU.min).then_inc(d_step, 1)
            dve.wait_ge(d_step, 1)
            dve.wait_ge(w_loaded, 16)
            v.tensor_scalar(wTs[:, :], wT_in[:, :], dcol[:, 1:2], DT, ALU.mult, ALU.mult).then_inc(d_step, 1)
            dve.wait_ge(gate_exp, 1)
            v.tensor_scalar(esum[:, :, 1], esum[:, :, 0], 1.0, None, ALU.add).then_inc(gate_step, 1)
            dve.wait_ge(gate_step, 1)
            v.reciprocal(esum[:, :, 2], esum[:, :, 1]).then_inc(gate_step, 1)
            dve.wait_ge(gate_step, 2)
            v.tensor_scalar(gcol[:, :], esum[:, :, 2], 0.5 * DT, None, ALU.mult).then_inc(gate_step, 1)
            v.tensor_scalar(ccol[:, :], esum[:, :, 2], -0.5 * DT, 1.0 - DT, ALU.mult, ALU.add).then_inc(gate_step, 1)
            dve.wait_ge(gate_step, 4)
            for t in range(NT):
                dve.wait_ge(adj_loaded[t], 16)
                v.tensor_scalar(A[:, t, :].rearrange("p (b a) -> p b a", b=NT),
                                       adj_in[:, t, :].rearrange("p (a b) -> p b a", b=NT),
                                gcol[:, t:t + 1], None, ALU.mult).then_inc(a_step, 1)
                dve.wait_ge(a_step, t + 1)
                v.scalar_tensor_tensor(A[:, t, t * P:(t + 1) * P], ident[:, :], ccol[:, t:t + 1],
                                       A[:, t, t * P:(t + 1) * P], ALU.mult, ALU.add).then_inc(a_ready, 1)

            def a_turned(g):
                for mt in range(NT):
                    dve.wait_ge(t_high, mt + 1)
                    v.tensor_tensor(TA[0][1][:, mt, :], (left + right)[mt][:, :], f32(TA[0][0][:, mt, :]),
                                    ALU.subtract).then_inc(t_low, 1)

            def a_split(g):
                for t in range(NT):
                    dve.wait_ge(a_high, t + 1)
                    v.tensor_tensor(As[1][:, t, :], A[:, t, :], f32(As[0][:, t, :]),
                                    ALU.subtract).then_inc(a_low, 1)

            def power2(g, mt):
                dve.wait_ge(t_high, NT + mt + 1)
                v.tensor_tensor(TA[1][1][:, mt, :], A2_BANKS[mt], f32(TA[1][0][:, mt, :]),
                                ALU.subtract).then_inc(t_low, 1)

            def r_sum(g, p):
                dve.wait_ge(cp_copied, 2 if p == 1 else 3 if p == 2 else 4 if p < 5 else 5)
                dve.wait_ge(r_level, p)
                for k in range(STEPS - p):
                    acc = RF[:, k % I3, k // I3, :]
                    last = v.scalar_tensor_tensor(acc, CP[:, p, :], DT * comb(k + p, k),
                                                  identdt[:, :] if p == 1 else acc, ALU.mult, ALU.add)
                last.then_inc(r_level, 1)

            def r_all(g):
                dve.wait_ge(r_level, STEPS)
                dve.wait_ge(fc_made, 3)
                dve.wait_ge(q_made, 1)
                for k in range(STEPS + 1):
                    p = STEPS - k
                    acc = RF[:, k % I3, k // I3, :]
                    fc = wide[:, p // 4, (p % 4) * D:(p % 4 + 1) * D] if p < STEPS else turn[:, 0:D]
                    if k == STEPS:
                        last = v.tensor_copy(acc, fc)
                    else:
                        last = v.scalar_tensor_tensor(acc, fc, float(comb(STEPS, k)),
                                                      acc if k < STEPS - 1 else identdt[:, :], ALU.mult, ALU.add)
                last.then_inc(r_level, 1)
                dve.wait_ge(rc_high, 1)
                v.tensor_tensor(RC[1][:, :, :], RF[:, :, :, :].rearrange("p i j d -> p i (j d)"),
                                f32(RC[0][:, :, :]), ALU.subtract).then_inc(rc_low, 1)

            def vec_split(r):
                dve.wait_ge(v_step, 3 * r + 1)
                v.tensor_copy(Vs[:, r, :, 0:NV], V[:, :, NV * r:NV * r + NV]).then_inc(v_step, 1)
                dve.wait_ge(v_step, 3 * r + 2)
                v.tensor_tensor(Vs[:, r, :, NV:2 * NV], V[:, :, NV * r:NV * r + NV], f32(Vs[:, r, :, 0:NV]),
                                ALU.subtract).then_inc(v_step, 1)

            def power3(g, mt):
                dve.wait_ge(t_high, 2 * NT + mt + 1)
                v.tensor_tensor(TA[2][1][:, mt, :], wide[:, mt % 2, :], f32(TA[2][0][:, mt, :]),
                                ALU.subtract).then_inc(t_low, 1)
                if mt == 0:
                    v.tensor_reduce(s1[:, :], adj_in, AX.X, ALU.add).then_inc(rowsum_done, 1)
                    v.tensor_tensor(fold[:, :], ident[0:2 * NV, 0:NV], ident[0:2 * NV, NV:2 * NV], ALU.add)
                    v.memset(V[:, :, :], 1.0).then_inc(rowsum_done, 1)
                    v.memset(Qc[:, :, :, :], 0.0).then_inc(rowsum_done, 1)
                    dve.wait_ge(rowsum_done, 3)
                    v.tensor_tensor(V[:, :, 1], s1[:, :], gcol[:, :], ALU.mult).then_inc(rowsum_done, 1)
                    v.tensor_tensor(s2[:, :], s1[:, :], s1[:, :], ALU.mult)
                    dve.wait_ge(rowsum_done, 4)
                    v.tensor_tensor(V[:, :, 1], V[:, :, 1], ccol[:, :], ALU.add).then_inc(rowsum_done, 1)
                    dve.wait_ge(rowsum_done, 5)
                    v.tensor_copy(Vs[:, 1, :, 0:NV], V[:, :, 0:NV]).then_inc(rowsum_done, 1)
                    dve.wait_ge(rowsum_done, 6)
                    v.tensor_tensor(Vs[:, 1, :, NV:2 * NV], V[:, :, 0:NV], f32(Vs[:, 1, :, 0:NV]),
                                    ALU.subtract).then_inc(rowsum_done, 1)
                    dve.wait_ge(q_made, 1)
                    for k in range(STEPS + 1):
                        src = turn[:, D + STEPS - k:D + STEPS - k + 1]
                        for part in range(2):
                            last = v.tensor_scalar(Qc[:, k // I3, part, k % I3:k % I3 + 1], src,
                                                   float(comb(STEPS, k)), None, ALU.mult)
                    last.then_inc(q_scaled, 1)

            def vec(g, r):
                dve.wait_ge(v_made, r + 1)
                v.tensor_copy(Vrow[:, VROW[r], :], wide[0:2 * NV, r % 2, :]).then_inc(v_rows, 1)

            def vec_back(g, r):
                dve.wait_ge(v_back, r + 1)
                made = turn[:, 256 + 64 * r:256 + 64 * r + NT * NV].rearrange("p (t c) -> p t c", t=NT)
                if r == 0:
                    v.tensor_copy(V[:, :, 2], made[:, :, 1]).then_inc(v_step, 1)
                else:
                    v.tensor_copy(V[:, :, NV * r:NV * r + NV], made).then_inc(v_step, 1)
                vec_split(r)

            def vecT(g):
                dve.wait_ge(q_turned, 1)
                v.tensor_copy(Qrow[:, :, :].rearrange("k j d -> k (j d)"),
                              turn[0:2 * NV, 0:I3 * D]).then_inc(q_copied, 1)
                dve.wait_ge(v_turned, 1)
                v.tensor_copy(Vrow[0:NV, 0, :], wide[0:NV, 1, :]).then_inc(v_copied, 1)

            def bias_part(g):
                dve.wait_ge(gb_made, 1)
                v.tensor_copy(g_bias[:, :, :].rearrange("p t d -> p (t d)"), wide[:, 1, :]).then_inc(gb_copied, 1)

            def soft(g, t):
                dve.wait_ge(z_made, t + 1)
                if t >= 1:
                    dve.wait_ge(z_exp, t)
                v.tensor_scalar(relu[:, :], tail[:, :], 0.0, None, ALU.max).then_inc(relu_done, 1)
                dve.wait_ge(relu_done, t + 1)
                v.tensor_reduce(zmax[:, t:t + 1], relu[:, :], AX.X, ALU.max).then_inc(a_step, 1)
                dve.wait_ge(a_step, NT + t + 1)
                v.tensor_scalar(zneg[:, t:t + 1], zmax[:, t:t + 1], -1.0, None, ALU.mult).then_inc(zneg_done, 1)
                dve.wait_ge(z_exp, t + 1)
                v.reciprocal(zrec[:, t:t + 1], zsum[:, t:t + 1]).then_inc(zrec_done, 1)

            def coef(g):
                dve.wait_ge(bout_loaded, 16)
                dve.wait_ge(a_done, NT)
                v.tensor_tensor(a2[:, :], a1[:, :], a1[:, :], ALU.mult).then_inc(coef_done, 1)

            def y_low(i):
                def stage(g, b):
                    dve.wait_ge(yT_high, y_use(i, b, g) + 1)
                    v.tensor_tensor(yT[i][1][:, b % 2, :], left_bank((f"y{i}", b), g)[:, :],
                                    f32(yT[i][0][:, b % 2, :]), ALU.subtract).then_inc(left_drained, 1)
                return stage

            def inner(g, b, t):
                at = NT * (GB * g + b) + t
                bank = right[t % 2]
                dve.wait_ge(inner_mid, at + 1)
                v.tensor_tensor(Z0[:, t, b, :], bank[:, 0:D], x_in[:, b, t * D:(t + 1) * D],
                                ALU.add).then_inc(inner_base, 1)
                v.tensor_tensor(Z2[1][:, t, b * D:(b + 1) * D], bank[:, 2 * D:3 * D],
                                f32(Z2[0][:, t, b * D:(b + 1) * D]), ALU.subtract).then_inc(inner_low, 1)

            def outer1(g, t):
                dve.wait_ge(o1_made, NT * (g - 1) + t + 1)
                dve.wait_ge(inner_mid, NT * GB * g)
                z1 = Z1[:, t, :, :].rearrange("p b d -> p (b d)")
                v.tensor_tensor(z1, left_bank(("O1", t), g)[:, :], z1, ALU.add).then_inc(left_drained, 1)

            def stats(ln, src, u, step, at):
                for b in range(GB):
                    last = v.bn_stats(ln["st"][:, u % 2, b, :], src[:, b, :])
                last.then_inc(step, 1)
                dve.wait_ge(step, at + 1)
                dve.sem_inc(stats_seen)
                for b in range(GB):
                    last = v.bn_aggr(ln["mv"][:, u % 2, b, :], ln["st"][:, u % 2, b, :])
                last.then_inc(step, 1)

            def rsqrt(ln, u, step, at):
                s = u % 2
                r0, q, mv = ln["r0"][:, s, :], ln["q"][:, s, :], ln["mv"][:, s, :, :]
                v.reciprocal(r0, ln["sd"][:, s, :]).then_inc(step, 1)
                dve.wait_ge(step, at + 1)
                v.scalar_tensor_tensor(q, mv[:, :, 1], EPS, r0, ALU.add, ALU.mult).then_inc(step, 1)
                dve.wait_ge(step, at + 2)
                v.scalar_tensor_tensor(ln["q2"][:, s, :], q, -0.5, r0, ALU.mult, ALU.mult).then_inc(step, 1)
                dve.wait_ge(step, at + 3)
                v.scalar_tensor_tensor(ln["r"][:, s, :], ln["q2"][:, s, :], 1.5, r0,
                                       ALU.add, ALU.mult).then_inc(step, 1)
                dve.wait_ge(step, at + 4)
                v.scalar_tensor_tensor(ln["nb"][:, s, :], mv[:, :, 0], -1.0, ln["r"][:, s, :],
                                       ALU.mult, ALU.mult).then_inc(step, 1)

            def outer2(g, u):
                q = NT * (g - 1) + u
                dve.wait_ge(o2_made, q + 1)
                dve.wait_ge(base_full, q + 1)
                v.tensor_tensor(x2[:, u, :, :].rearrange("p b d -> p (b d)"), left_bank(("O2", u), g)[:, :],
                                Z0[:, u, :, :].rearrange("p b d -> p (b d)"), ALU.add).then_inc(left_drained, 1)

            def stat1(g, u):
                dve.wait_ge(left_drained, left_use(("O2", u), g) + 1)
                stats(LN[0], x2[:, u, :, :], u, ln1_stat, STAT * (NT * (g - 1) + u))

            def norm1(g, u):
                q = NT * (g - 1) + u
                dve.wait_ge(ln1_root, q + 1)
                rsqrt(LN[0], u, ln1_norm, NORM * q)

            def turned(g, u):
                dve.wait_ge(x2T_high, NT * (g - 1) + u + 1)
                v.tensor_tensor(x2T[1][:, u % 2, :, :].rearrange("p b d -> p (b d)"), turn[:, :],
                                f32(x2T[0][:, u % 2, :, :].rearrange("p b d -> p (b d)")),
                                ALU.subtract).then_inc(x2T_low, 1)

            def mix(g, u, half):
                at = 2 * (NT * (g - 1) + u) + half
                r = res[:, u % 2, 2 * half:2 * half + 2, :]
                if u >= 2 and half == 0:
                    dve.wait_ge(out_ready, NT * (g - 1) + u - 1)
                dve.wait_ge(wide_made, at + 1)
                pair = MIX_BANKS[mix_set(g, half)][0]
                v.tensor_tensor(r, pair[:, :, 0:D], bias_out[:, :, :], ALU.add).then_inc(mixed, 1)
                for n, factor in ((1, s1), (2, s2)):
                    dve.wait_ge(mixed, MIX * at + n)
                    v.scalar_tensor_tensor(r, pair[:, :, n * D:(n + 1) * D], factor[:, u:u + 1], r,
                                           ALU.mult, ALU.add).then_inc(mixed, 1)

            def stat2(g, u):
                q = NT * (g - 1) + u
                dve.wait_ge(res_full, 2 * (q + 1))
                stats(LN[1], res[:, u % 2, :, :], u, ln2_stat, STAT * q)

            def norm2(g, u):
                q = NT * (g - 1) + u
                dve.wait_ge(ln2_root, q + 1)
                rsqrt(LN[1], u, ln2_norm, NORM * q)
            run(dve, {"AT": a_turned, "A": a_split, "A2": power2, "Rsum": r_sum, "RC": r_all,
                      "A3": power3, "vec": vec, "vback": vec_back, "vecT": vecT, "gbias": bias_part, "soft": soft,
                      "coef": coef, "y1": y_low(1), "y2": y_low(2), "R": inner, "O1": outer1,
                      "O2": outer2, "stat1": stat1, "norm1": norm1, "T": turned, "W": mix,
                      "stat2": stat2, "norm2": norm2})

        @block.tensor
        def _(pe):
            pe.wait_ge(d_step, 2)
            pe.matmul(turn[:, 0:D], wTs[:, :], wT_in[:, :], start=True, stop=True).then_inc(cp_made, 1)
            pe.wait_ge(cp_copied, 2)
            pe.matmul(turn[:, D:2 * D], CP[:, 1, :], CP[:, 1, :], start=True, stop=True).then_inc(cp_made, 1)

            def c34(g):
                pe.wait_ge(cp_copied, 3)
                pe.matmul(turn[:, 2 * D:4 * D], CP[:, 2, :], CP[:, 1:3, :].rearrange("p k d -> p (k d)"),
                          start=True, stop=True).then_inc(cp_made, 1)

            def c58(g):
                pe.wait_ge(cp_copied, 4)
                pe.matmul(tail[:, :], CP[:, 4, :], CP[:, 1:5, :].rearrange("p k d -> p (k d)"),
                          start=True, stop=True).then_inc(cp_made, 1)

            def a_turned(g):
                for t in range(NT):
                    pe.wait_ge(a_ready, t + 1)
                    for mt in range(NT):
                        turned_a = pe.transpose((left + right)[mt][:, t * P:(t + 1) * P],
                                                A[:, t, mt * P:(mt + 1) * P], ident[:, :])
                        if t == NT - 1:
                            turned_a.then_inc(at_turned, 1)

            def fc(g):
                pe.wait_ge(cp_copied, 5)
                pe.wait_ge(fcw_loaded, 16)
                pe.wait_ge(t_low, 2 * NT)
                for lo, hi, bank in ((0, 4, wide[:, 0, :]), (4, 8, wide[:, 1, :]), (8, 9, turn[:, 0:D])):
                    pe.matmul(bank, fcw_in[:, :], CP[:, lo:hi, :].rearrange("p k d -> p (k d)"),
                              start=True, stop=True).then_inc(fc_made, 1)
                pe.wait_ge(b_loaded, 16)
                for p in range(STEPS + 1):
                    last = pe.matmul(turn[:, D + p:D + p + 1], CP[:, p, :], b_in[:, :], start=True, stop=True)
                last.then_inc(q_made, 1)

            def power(k, mt, bank):
                for kt in range(NT):
                    if k == 2 and mt == 0:
                        pe.wait_ge(a_low, kt + 1)
                    last = three(pe, bank, [a[:, kt, mt * P:(mt + 1) * P] for a in As],
                                 [a[:, kt, :] for a in TA[k - 2]], kt == 0, kt == NT - 1)
                last.then_inc(t_made, 1)

            def power2(g, mt):
                power(2, mt, A2_BANKS[mt])

            def power3(g, mt):
                if mt == 0:
                    pe.wait_ge(t_low, 2 * NT)
                    pe.wait_ge(rc_high, 1)
                if mt >= 2:
                    pe.wait_ge(t_low, 2 * NT + mt - 1)
                power(3, mt, wide[:, mt % 2, :])

            def vec(g, r):
                if r == 0:
                    pe.wait_ge(rowsum_done, 7)
                    pe.wait_ge(q_scaled, 1)
                    pe.wait_ge(t_low, 2 * NT + 3)
                else:
                    pe.wait_ge(v_step, 3 * r)
                if r == 1:
                    pe.wait_ge(t_low, 3 * NT)
                src, mats = (1, TA[0]) if r == 0 else (r - 1, TA[2])
                for kt in range(NT):
                    pe.matmul(wide[0:2 * NV, r % 2, :], Vs[:, src, kt, :], mats[0][:, kt, :],
                              start=kt == 0, stop=False)
                    last = pe.matmul(wide[0:NV, r % 2, :], Vs[:, src, kt, 0:NV], mats[1][:, kt, :],
                                     start=False, stop=kt == NT - 1)
                last.then_inc(v_made, 1)

            def vec_back(g, r):
                pe.wait_ge(v_rows, r + 1)
                for t in range(NT):
                    o = 256 + 64 * r + NV * t
                    last = pe.matmul(turn[:, o:o + NV], Vrow[:, VROW[r], t * P:(t + 1) * P],
                                     fold[:, :], start=True, stop=True)
                last.then_inc(v_back, 1)

            def vecT(g):
                pe.wait_ge(v_step, 6)
                for j in range(I3):
                    last = pe.transpose(turn[0:2 * NV, j * D:(j + 1) * D],
                                        Qc[:, j, :, :].rearrange("p a c -> p (a c)"), ident[:, :])
                last.then_inc(q_turned, 1)
                for t in range(NT):
                    last = pe.transpose(wide[0:NV, 1, t * P:(t + 1) * P], V[:, t, 0:NV], ident[:, :])
                last.then_inc(v_turned, 1)

            def bias_part(g):
                pe.wait_ge(q_copied, 1)
                pe.wait_ge(v_copied, 1)
                pe.wait_ge(v_rows, 3)
                for t in range(NT):
                    for j in range(I3):
                        rows = 2 * NV if j else NV
                        last = pe.matmul(wide[:, 1, t * D:(t + 1) * D], Vrow[0:rows, j, t * P:(t + 1) * P],
                                         Qrow[0:rows, j, :], start=j == 0, stop=j == I3 - 1)
                last.then_inc(gb_made, 1)

            def soft(g, t):
                if t == 0:
                    pe.wait_ge(nv_loaded, 32)
                else:
                    pe.wait_ge(relu_done, t)
                pe.matmul(tail[:, :], nv1_in[:, t, :], nv2_in[:, :], start=True, stop=True).then_inc(z_made, 1)

            def left_free(stage, g):
                use = left_use(stage, g)
                if isinstance(use, int) and use < 2:
                    return
                pe.wait_ge(left_drained, use if is_last(g) and stage == ("O2", NT - 1) else use - 1)

            def y(i):
                def stage(g, b):
                    pe.wait_ge(xs_low, GB * g + b + 1)
                    left_free((f"y{i}", b), g)
                    for kt in range(NT):
                        if isinstance(g, int) and b == 0:
                            pe.wait_ge(t_low, NT * (i - 1) + kt + 1)
                        last = three(pe, left_bank((f"y{i}", b), g)[:, :], [a[:, b % 2, kt, :] for a in xs],
                                     [a[:, kt, :] for a in TA[i - 1]], kt == 0, kt == NT - 1)
                    last.then_inc(y_made, 1)
                return stage

            def inner(g, b, t):
                at = NT * (GB * g + b) + t
                if t == 0:
                    pe.wait_ge(xts_low, GB * g + b + 1)
                    pe.wait_ge(left_drained, left_use(("y2", b), g) + 1)
                if isinstance(g, int) and b == 0 and t == 0:
                    pe.wait_ge(rc_low, 1)
                if not (isinstance(at, int) and at < 2):
                    pe.wait_ge(inner_low, at - 1)
                for i in range(I3):
                    last = three(pe, right[t % 2][:, 0:J3 * D], [a[:, b % 2, t * P:(t + 1) * P] for a in yT[i]],
                                 [a[:, i, :] for a in RC], i == 0, i == I3 - 1)
                last.then_inc(right_made, 1)

            def outer(moving, made, name):
                def stage(g, t):
                    left_free((name, t), g)
                    for kt in range(NT):
                        if t == 0 and name == "O1":
                            pe.wait_ge(inner_low, NT * (GB * g - 1) + kt + 1)
                        if t == 0 and name == "O2":
                            pe.wait_ge(u_low, NT * (g - 1) + kt + 1)
                        last = three(pe, left_bank((name, t), g)[:, :],
                                     [a[:, kt, t * P:(t + 1) * P] for a in TA[2]],
                                     [a[:, kt, :] for a in moving], kt == 0, kt == NT - 1)
                    last.then_inc(made, 1)
                return stage

            def turned(g, u):
                q = NT * (g - 1) + u
                pe.wait_ge(x2_ready, q + 1)
                if u:
                    pe.wait_ge(x2T_low, q)
                for b in range(GB):
                    last = pe.transpose(turn[:, b * P:(b + 1) * P], x2[:, u, b, :], ident[:, :])
                last.then_inc(turn_made, 1)

            def mix(g, u, half):
                q = NT * (g - 1) + u
                pe.wait_ge(x2T_low, q + 1)
                if u or (half and not is_last(g)):
                    pe.wait_ge(mixed, MIX * mix_before(g, 2 * q + half))
                    pe.wait_ge(tail_taken, mix_before(g, 2 * q + half))
                elif half:
                    pe.wait_ge(left_drained, left_use(("O2", NT - 3), g) + 1)
                if u == 0 and half == 0:
                    pe.wait_ge(wc_low, 1)
                pair, tail_v = MIX_BANKS[mix_set(g, half)]
                for t in range(2):
                    weights = [a[:, u % 2, 2 * half + t, :] for a in x2T]
                    three(pe, pair[:, t, 0:PW], weights, [a[:, 0:PW] for a in WC], True, True)
                    last = three(pe, tail_v[:, t, :], weights, [a[:, PW:NP5 * D] for a in WC], True, True)
                last.then_inc(wide_made, 1)

            run(pe, {"C34": c34, "C58": c58, "AT": a_turned, "FC": fc, "A2": power2,
                     "A3": power3, "vec": vec, "vback": vec_back, "vecT": vecT, "gbias": bias_part, "soft": soft,
                     "y1": y(1), "y2": y(2), "R": inner, "O1": outer(Z2, o1_made, "O1"),
                     "O2": outer(U, o2_made, "O2"), "T": turned, "W": mix})


def kernel(x, adj, L0_gnn_alpha_train, L0_gnn_w, L0_gnn_d, L0_gnn_fc_in_w, L0_gnn_fc_in_b,
           L1_gnn_node_vec1, L1_gnn_node_vec2, L1_gnn_W, L1_gnn_b):
    import numpy as np
    import concourse.bacc as bacc
    from concourse.bass_utils import run_bass_kernel_spmd

    B, N, D = x.shape
    T = 4
    x, nv1 = np.asarray(x), np.asarray(L1_gnn_node_vec1)
    arrays = {
        "x": x,
        "xT": x.reshape(B, N // T, T, D).transpose(0, 3, 2, 1).reshape(B, D, N),
        "adj": adj,
        "alpha": L0_gnn_alpha_train,
        "wT": np.asarray(L0_gnn_w).T,
        "dvec": L0_gnn_d,
        "fcw": L0_gnn_fc_in_w,
        "bin": L0_gnn_fc_in_b,
        "nv1T": nv1.reshape(N // T, T, nv1.shape[1]).transpose(2, 1, 0).reshape(nv1.shape[1], N),
        "nv2": L1_gnn_node_vec2,
        "W": L1_gnn_W,
        "bout": np.broadcast_to(np.asarray(L1_gnn_b), (128, 2, D)).reshape(128, 2 * D),
    }
    nc = bacc.Bacc("TRN2", target_bir_lowering=False, num_devices=1)
    feeds, args = {}, []
    for name, a in arrays.items():
        a = np.ascontiguousarray(a)
        feeds[f"in_{name}"] = a
        args.append(nc.dram_tensor(f"in_{name}", a.shape, mybir.dt.from_np(a.dtype), kind="ExternalInput").ap())
    args.append(nc.dram_tensor("out", (B, N, D), mybir.dt.float32, kind="ExternalOutput").ap())
    graph_resnorm_kernel(nc, *args)
    r = run_bass_kernel_spmd(nc, [feeds], core_ids=[0])
    return r.results[0]["out"]
```
